# Optimizing a Trainium2 kernel written in Bass

```python
import numpy as np
import jax
import jax.numpy as jnp

def _softmax(x, axis=-1):
    return jax.nn.softmax(x, axis=axis)
def _gelu(x):
    return jax.nn.gelu(x, approximate=True)
def _silu(x):
    return jax.nn.silu(x)
def _sigmoid(x):
    return jax.nn.sigmoid(x)
def _layernorm(x, axis=-1, eps=1e-5):
    m = jnp.mean(x, axis=axis, keepdims=True)
    v = jnp.var(x, axis=axis, keepdims=True)
    return (x - m) / jnp.sqrt(v + eps)
def _scatter_add(tgt, idx, src, axis=0):
    return tgt.at[idx].add(src)
def _segment_sum(src, seg, n):
    return jax.ops.segment_sum(src, seg, n)

kernel_name = 'mk_adj_preln_d4_adj_128_697735'

def setup_inputs(seed: int = 0):
    np.random.seed(seed)
    _w = jnp.asarray
    def _rec_inputs():
        import jax
        import jax.numpy as jnp
        _gk = jax.random.key(seed)
        x = -0.000929 + 1 * jax.random.normal(jax.random.fold_in(_gk, 1), (16, 1024, 128), jnp.float32)
        _w = (1.0 + jnp.arange(1024, dtype=jnp.float32)) ** -0.5
        _w = _w / _w.mean()
        _pij = jnp.clip(0.03125 * _w[:, None] * _w[None, :], 0.0, 1.0)
        _a = jax.random.uniform(jax.random.fold_in(_gk, 2), (16, 1024, 1024)) < _pij
        adj = _a.astype(jnp.int32)
        return x, adj
    x, adj = _rec_inputs()
    def _L0_gnn_setup():
        import jax, jax.numpy as jnp
        import numpy as np
        BN_EPS = 0.001
        NEG_INF = -1e+30

        def _masked_row_softmax(adjT):
            mask = adjT != 0
            logits = jnp.where(mask, adjT, NEG_INF)
            p = jax.nn.softmax(logits, axis=-1)
            return jnp.where(mask, p, 0.0)

        def _batch_norm(x, gamma, beta):
            mean = jnp.mean(x, axis=(0, 1), keepdims=True)
            var = jnp.var(x, axis=(0, 1), keepdims=True)
            return (x - mean) * jax.lax.rsqrt(var + BN_EPS) * gamma + beta
        key = jax.random.key(seed)
        ks = jax.random.split(key, 4)
        B, N, F = (1, 8192, 128)
        C0, C1 = (256, 128)
        features = jax.random.normal(ks[0], (B, N, F), dtype=jnp.float32)
        adj = jax.random.randint(ks[1], (B, N, N), 0, 2, dtype=jnp.int32)
        kernel_1 = jax.random.normal(ks[2], (F, C0), dtype=jnp.float32) * (1.0 / np.sqrt(F))
        kernel_2 = jax.random.normal(ks[3], (C0, C1), dtype=jnp.float32) * (1.0 / np.sqrt(C0))
        return {'features': features, 'adj': adj, 'kernel_1': kernel_1, 'bias_1': jnp.zeros((C0,), jnp.float32), 'gamma_1': jnp.ones((C0,), jnp.float32), 'beta_1': jnp.zeros((C0,), jnp.float32), 'kernel_2': kernel_2, 'bias_2': jnp.zeros((C1,), jnp.float32), 'gamma_2': jnp.ones((C1,), jnp.float32), 'beta_2': jnp.zeros((C1,), jnp.float32)}
    _L0_gnn_all = _L0_gnn_setup()
    _L0_gnn_in = {k: v for k, v in _L0_gnn_all.items() if k in ('kernel_1', 'bias_1', 'gamma_1', 'beta_1', 'kernel_2', 'bias_2', 'gamma_2', 'beta_2', )}
    del _L0_gnn_all

    def _L1_gnn_setup():
        import jax, jax.numpy as jnp
        import numpy as np
        IN_DIM = 128
        OUT_DIM = 128
        B, N = (8, 2048)
        NEG_SLOPE = 0.2
        key = jax.random.key(seed)
        k_h, k_adj, k_W, k_a = jax.random.split(key, 4)
        h = jax.random.normal(k_h, (B, N, IN_DIM), dtype=jnp.float32)
        adj = jax.random.randint(k_adj, (B, N, N), 0, 2, dtype=jnp.int32)
        W = jax.random.normal(k_W, (OUT_DIM, IN_DIM), dtype=jnp.float32) * (1.0 / np.sqrt(IN_DIM))
        a = jax.random.normal(k_a, (2 * OUT_DIM,), dtype=jnp.float32) * (1.0 / np.sqrt(2 * OUT_DIM))
        return {'h': h, 'adj': adj, 'W': W, 'a': a}
    _L1_gnn_all = _L1_gnn_setup()
    _L1_gnn_in = {k: v for k, v in _L1_gnn_all.items() if k in ('W', 'a', )}
    del _L1_gnn_all

    def _L2_gnn_setup():
        import jax, jax.numpy as jnp
        import numpy as np
        B, N, D = (256, 50, 128)
        NEG = -9000000000000000.0
        LEAKY_SLOPE = 0.2
        key = jax.random.key(seed)
        ks = jax.random.split(key, 6)
        hidden = jax.random.normal(ks[0], (B, N, D), dtype=jnp.float32)
        adj = jax.random.randint(ks[1], (B, N, N), 0, 5)
        a_0 = jax.random.normal(ks[2], (D, 1), dtype=jnp.float32) * 0.05
        a_1 = jax.random.normal(ks[3], (D, 1), dtype=jnp.float32) * 0.05
        a_2 = jax.random.normal(ks[4], (D, 1), dtype=jnp.float32) * 0.05
        a_3 = jax.random.normal(ks[5], (D, 1), dtype=jnp.float32) * 0.05
        return {'hidden': hidden, 'adj': adj, 'a_0': a_0, 'a_1': a_1, 'a_2': a_2, 'a_3': a_3}
    _L2_gnn_all = _L2_gnn_setup()
    _L2_gnn_in = {k: v for k, v in _L2_gnn_all.items() if k in ('a_0', 'a_1', 'a_2', 'a_3', )}
    del _L2_gnn_all

    def _L3_gnn_setup():
        import jax, jax.numpy as jnp
        import numpy as np
        NEG_BIG = -9000000000000000.0
        ALPHA = 0.2
        key = jax.random.key(seed)
        k1, k2, k3, k4 = jax.random.split(key, 4)
        B, N, F_in, F_out = (8, 2048, 128, 128)
        h = jax.random.normal(k1, (B, N, F_in), dtype=jnp.float32)
        adj = jax.random.randint(k2, (B, N, N), 0, 2, dtype=jnp.int32)

        def xavier(k, shape, gain=1.414):
            fan_in, fan_out = (shape[0], shape[1])
            bound = gain * np.sqrt(6.0 / (fan_in + fan_out))
            return jax.random.uniform(k, shape, jnp.float32, -bound, bound)
        W = xavier(k3, (F_in, F_out))
        a = xavier(k4, (2 * F_out, 1))
        return {'h': h, 'adj': adj, 'W': W, 'a': a}
    _L3_gnn_all = _L3_gnn_setup()
    _L3_gnn_in = {k: v for k, v in _L3_gnn_all.items() if k in ('W', 'a', )}
    del _L3_gnn_all

    return {
        "x": x,
        "adj": adj,
        "L0_gnn_kernel_1": _L0_gnn_in["kernel_1"],
        "L0_gnn_bias_1": _L0_gnn_in["bias_1"],
        "L0_gnn_gamma_1": _L0_gnn_in["gamma_1"],
        "L0_gnn_beta_1": _L0_gnn_in["beta_1"],
        "L0_gnn_kernel_2": _L0_gnn_in["kernel_2"],
        "L0_gnn_bias_2": _L0_gnn_in["bias_2"],
        "L0_gnn_gamma_2": _L0_gnn_in["gamma_2"],
        "L0_gnn_beta_2": _L0_gnn_in["beta_2"],
        "L1_gnn_W": _L1_gnn_in["W"],
        "L1_gnn_a": _L1_gnn_in["a"],
        "L2_gnn_a_0": _L2_gnn_in["a_0"],
        "L2_gnn_a_1": _L2_gnn_in["a_1"],
        "L2_gnn_a_2": _L2_gnn_in["a_2"],
        "L2_gnn_a_3": _L2_gnn_in["a_3"],
        "L3_gnn_W": _L3_gnn_in["W"],
        "L3_gnn_a": _L3_gnn_in["a"],
    }

def reference(x, adj, L0_gnn_kernel_1, L0_gnn_bias_1, L0_gnn_gamma_1, L0_gnn_beta_1, L0_gnn_kernel_2, L0_gnn_bias_2, L0_gnn_gamma_2, L0_gnn_beta_2, L1_gnn_W, L1_gnn_a, L2_gnn_a_0, L2_gnn_a_1, L2_gnn_a_2, L2_gnn_a_3, L3_gnn_W, L3_gnn_a):
    import jax
    import jax.numpy as jnp
    def _L0_gnn_ref(features, adj, kernel_1, bias_1, gamma_1, beta_1, kernel_2, bias_2, gamma_2, beta_2):
        import jax, jax.numpy as jnp
        import numpy as np
        BN_EPS = 0.001
        NEG_INF = -1e+30

        def _masked_row_softmax(adjT):
            mask = adjT != 0
            logits = jnp.where(mask, adjT, NEG_INF)
            p = jax.nn.softmax(logits, axis=-1)
            return jnp.where(mask, p, 0.0)

        def _batch_norm(x, gamma, beta):
            mean = jnp.mean(x, axis=(0, 1), keepdims=True)
            var = jnp.var(x, axis=(0, 1), keepdims=True)
            return (x - mean) * jax.lax.rsqrt(var + BN_EPS) * gamma + beta
        adjT = jnp.transpose(adj.astype(jnp.float32), (0, 2, 1))
        w = _masked_row_softmax(adjT)
        region = jnp.matmul(w, features)
        region = jnp.matmul(region, kernel_1) + bias_1
        region = _batch_norm(region, gamma_1, beta_1)
        people = jnp.matmul(jnp.transpose(w, (0, 2, 1)), region)
        people = jnp.matmul(people, kernel_2) + bias_2
        people = _batch_norm(people, gamma_2, beta_2)
        return people

    def _L1_gnn_ref(h, adj, W, a):
        import jax, jax.numpy as jnp
        import numpy as np
        IN_DIM = 128
        OUT_DIM = 128
        B, N = (8, 2048)
        NEG_SLOPE = 0.2
        Wh = jnp.einsum('bnf,of->bno', h, W)
        Fo = Wh.shape[-1]
        a_src, a_dst = (a[:Fo], a[Fo:])
        s = Wh @ a_src
        t = Wh @ a_dst
        e = jax.nn.leaky_relu(s[:, :, None] + t[:, None, :], negative_slope=NEG_SLOPE)
        e = jnp.where(adj == 0, -jnp.inf, e)
        alpha = jax.nn.softmax(e, axis=-1)
        alpha = jnp.nan_to_num(alpha, nan=0.0)
        return jnp.einsum('bnm,bmo->bno', alpha, Wh)

    def _L2_gnn_ref(hidden, adj, a_0, a_1, a_2, a_3):
        import jax, jax.numpy as jnp
        import numpy as np
        B, N, D = (256, 50, 128)
        NEG = -9000000000000000.0
        LEAKY_SLOPE = 0.2
        A = jnp.concatenate([a_0, a_1, a_2, a_3], axis=1)
        e = jnp.einsum('bid,bjd,dk->bkij', hidden, hidden, A)
        e = jax.nn.leaky_relu(e, negative_slope=LEAKY_SLOPE)
        scores = jnp.full_like(e[:, 0], NEG)
        scores = jnp.where(adj == 1, e[:, 0], scores)
        scores = jnp.where(adj == 2, e[:, 1], scores)
        scores = jnp.where(adj == 3, e[:, 2], scores)
        scores = jnp.where(adj == 4, e[:, 3], scores)
        attn = jax.nn.softmax(scores, axis=-1)
        return jnp.einsum('bij,bjd->bid', attn, hidden)

    def _L3_gnn_ref(h, adj, W, a):
        import jax, jax.numpy as jnp
        import numpy as np
        NEG_BIG = -9000000000000000.0
        ALPHA = 0.2
        Wh = jnp.einsum('bnf,fo->bno', h, W)
        F_out = W.shape[1]
        a1 = a[:F_out, 0]
        a2 = a[F_out:, 0]
        s1 = Wh @ a1
        s2 = Wh @ a2
        e = jax.nn.leaky_relu(s1[:, :, None] + s2[:, None, :], negative_slope=ALPHA)
        e = jnp.where(adj > 0, e, NEG_BIG)
        attn = jax.nn.softmax(e, axis=-1)
        h_prime = jnp.einsum('bij,bjo->bio', attn, Wh)
        return jax.nn.elu(h_prime)

    h = jnp.maximum(_layernorm(x, axis=-1), 0.0)
    x = x + _L0_gnn_ref(h, adj, L0_gnn_kernel_1, L0_gnn_bias_1, L0_gnn_gamma_1, L0_gnn_beta_1, L0_gnn_kernel_2, L0_gnn_bias_2, L0_gnn_gamma_2, L0_gnn_beta_2)
    h = jnp.maximum(_layernorm(x, axis=-1), 0.0)
    x = x + _L1_gnn_ref(h, adj, L1_gnn_W, L1_gnn_a)
    h = jnp.maximum(_layernorm(x, axis=-1), 0.0)
    x = x + _L2_gnn_ref(h, adj, L2_gnn_a_0, L2_gnn_a_1, L2_gnn_a_2, L2_gnn_a_3)
    h = jnp.maximum(_layernorm(x, axis=-1), 0.0)
    x = x + _L3_gnn_ref(h, adj, L3_gnn_W, L3_gnn_a)
    return x


_drawn_inputs = setup_inputs


def setup_inputs(seed=0):
    import zlib

    import numpy as np

    out = dict(_drawn_inputs(seed))
    spreads = {'L0_gnn_bias_1': (0.0, 0.8),
     'L0_gnn_gamma_1': (1.0, 0.2),
     'L0_gnn_beta_1': (0.0, 0.1),
     'L0_gnn_bias_2': (0.0, 0.8),
     'L0_gnn_gamma_2': (1.0, 0.2),
     'L0_gnn_beta_2': (0.0, 0.1)}
    factors = {'L2_gnn_a_0': 3.794}
    for name, (base, spread) in spreads.items():
        noise = np.random.default_rng([zlib.crc32(name.encode()), seed]).standard_normal(out[name].shape)
        drawn = base * np.exp(spread * noise) if base else spread * noise
        out[name] = jnp.asarray(drawn.astype(out[name].dtype))
    for name, factor in factors.items():
        out[name] = (out[name] * factor).astype(out[name].dtype)
    return out
```

```python
import concourse.bass as bass
from concourse import mybir
from contextlib import ExitStack


def gnn_stack_kernel(nc, x_in, adj, k1, b1, g1, be1, k2, b2, g2, be2,
                     w_l1, a_l1, a2_0, a2_1, a2_2, a2_3, w_l3, a_l3, out):
    fp32, i32 = mybir.dt.float32, mybir.dt.int32
    ALU = mybir.AluOpType
    ACT = mybir.ActivationFunctionType
    AXX = mybir.AxisListType.X

    P = 128
    B, N, D = x_in.shape
    T = N // P
    C0 = k1.shape[1]
    O2 = C0 // P
    HALF = 512
    CH = N // HALF
    LN_EPS, BN_EPS, SLOPE = 1e-5, 1e-3, 0.2
    NEG_SOFT, NEG_BIG = 1e30, 9e15

    x_v = x_in.rearrange("b (t p) d -> b p t d", p=P)
    out_v = out.rearrange("b (t p) d -> b p t d", p=P)
    adj_cols = adj.rearrange("b (t p) c -> b p t c", p=P)

    w_dram = nc.dram_tensor("w_scratch", (B, N, N), fp32).ap()
    y_dram = nc.dram_tensor("y_scratch", (B, T, P, O2, P), fp32).ap()
    pT_dram = nc.dram_tensor("pT_scratch", (B, P, N), fp32).ap()

    ctx = ExitStack()
    with ctx:
        def sb(name, shape, dt=fp32, stack=ctx):
            return stack.enter_context(nc.sbuf_tensor(name, shape, dt))

        def sem(name, stack=ctx):
            return stack.enter_context(nc.semaphore(name))

        ident = sb("ident", [P, P])
        ones = sb("ones", [P, P])
        k1_sb = sb("k1_sb", [P, C0])
        k2_sb = sb("k2_sb", [P, O2, P])
        b1_sb, g1_sb, be1_sb = sb("b1_sb", [P, O2]), sb("g1_sb", [P, O2]), sb("be1_sb", [P, O2])
        b2_sb, g2_sb, be2_sb = sb("b2_sb", [P, 1]), sb("g2_sb", [P, 1]), sb("be2_sb", [P, 1])
        w1_sb, w1T = sb("w1_sb", [P, P]), sb("w1T", [P, P])
        w3_sb, w3T = sb("w3_sb", [P, P]), sb("w3T", [P, P])
        a1_sb, a3_sb = sb("a1_sb", [P, 2]), sb("a3_sb", [P, 2])
        a2_sb = sb("a2_sb", [P, 4])
        a_rep = sb("a_rep", [P, 4, P])
        v_rep = sb("v_rep", [P, 4, P])
        mhalf = sb("mhalf", [P, T])
        ps = ctx.enter_context(nc.psum_tensor("ps", [P, 8, HALF], fp32))

        weights_in = sem("weights_in")
        ident_zero, ident_ready = sem("ident_zero"), sem("ident_ready")
        wT_made, wT_kept, reps_made = sem("wT_made"), sem("wT_kept"), sem("reps_made")
        v_made, prologue_done = sem("v_made"), sem("prologue_done")

        def pair(k):
            return ps[:, 2 * k:2 * k + 2, :].rearrange("p a b -> p (a b)")

        loads = [(k1_sb[:, :], k1), (k2_sb[:, :, :], k2.rearrange("(o p) d -> p o d", p=P)),
                 (b1_sb[:, :], b1.rearrange("(o p) -> p o", p=P)), (g1_sb[:, :], g1.rearrange("(o p) -> p o", p=P)),
                 (be1_sb[:, :], be1.rearrange("(o p) -> p o", p=P)),
                 (b2_sb[:, :], b2.rearrange("(p o) -> p o", o=1)), (g2_sb[:, :], g2.rearrange("(p o) -> p o", o=1)),
                 (be2_sb[:, :], be2.rearrange("(p o) -> p o", o=1)),
                 (w1_sb[:, :], w_l1), (w3_sb[:, :], w_l3),
                 (a1_sb[:, :], a_l1.rearrange("(o p) -> p o", p=P)),
                 (a3_sb[:, :], a_l3.rearrange("(o p) k -> p (o k)", p=P))] \
            + [(a2_sb[:, k:k + 1], a) for k, a in enumerate((a2_0, a2_1, a2_2, a2_3))]

        with nc.allow_non_contiguous_dma("small weight vectors"), nc.Block() as block:
            @block.sync
            def _(sp):
                for dst, src in loads:
                    sp.dma_start(dst, src).then_inc(weights_in, 16)

            @block.gpsimd
            def _(pool):
                pool.memset(ident[:, :], 0.0).then_inc(ident_zero, 1)
                pool.memset(mhalf[:, :], -0.5)
                pool.wait_ge(ident_zero, 1)
                pool.affine_select(out=ident[:, :], in_=ident[:, :], compare_op=ALU.not_equal, fill=1.0,
                                   base=0, pattern=[[-1, P]], channel_multiplier=1).then_inc(ident_ready, 1)

            @block.tensor
            def _(pe):
                pe.wait_ge(weights_in, 16 * len(loads))
                pe.wait_ge(ident_ready, 1)
                nc.tensor.transpose(ps[:, 0, 0:P], w1_sb[:, :], ident[:, :])
                nc.tensor.transpose(ps[:, 1, 0:P], w3_sb[:, :], ident[:, :]).then_inc(wT_made, 1)
                pe.wait_ge(wT_kept, 1)
                pe.wait_ge(reps_made, 1)
                nc.tensor.matmul(ps[:, 2, 0:2 * P], w1_sb[:, :], a_rep[:, 0:2, :], start=True, stop=True)
                nc.tensor.matmul(ps[:, 3, 0:2 * P], w3T[:, :], a_rep[:, 2:4, :], start=True, stop=True).then_inc(v_made, 1)

            @block.vector
            def _(dve):
                dve.memset(ones[:, :], 1.0)
                dve.wait_ge(weights_in, 16 * len(loads))
                dve.drain()
                for k, a in enumerate((a1_sb[:, 0:1], a1_sb[:, 1:2], a3_sb[:, 0:1], a3_sb[:, 1:2])):
                    last = nc.vector.tensor_scalar(a_rep[:, k, :], ones[:, :], a, None, ALU.mult)
                last.then_inc(reps_made, 1)
                dve.wait_ge(wT_made, 1)
                nc.vector.tensor_copy(w1T[:, :], ps[:, 0, 0:P])
                nc.vector.tensor_copy(w3T[:, :], ps[:, 1, 0:P]).then_inc(wT_kept, 1)
                dve.wait_ge(v_made, 1)
                nc.vector.tensor_copy(v_rep[:, 0:2, :], ps[:, 2, 0:2 * P].rearrange("p (k q) -> p k q", k=2))
                nc.vector.tensor_copy(v_rep[:, 2:4, :], ps[:, 3, 0:2 * P].rearrange("p (k q) -> p k q", k=2))

        any_ctx = ctx.enter_context(ExitStack())

        def asb(name, shape, dt=fp32):
            return sb("any_" + name, shape, dt, any_ctx)

        def asem(name):
            return sem("any_" + name, any_ctx)

        xg, hg, cen = asb("xg", [P, T, P]), asb("hg", [P, T, P]), asb("cen", [P, T, P])
        lstat, lmv, lrs = asb("lstat", [P, T, 6]), asb("lmv", [P, T, 2]), asb("lrs", [P, T])
        adj_i = asb("adj_i", [P, N], i32)
        val, msk, sco, pro, tmp = (asb(n, [P, N]) for n in ("val", "msk", "sco", "pro", "tmp"))
        proT = asb("proT", [P, T, P])
        whT = asb("whT", [P, P])
        yT = asb("yT", [P, O2, P])
        yn = asb("yn", [P, O2, P])
        stats1 = asb("stats1", [P, O2, B * T, 6])
        stats2 = asb("stats2", [P, B * CH, 6])
        mv1, rs1 = asb("mv1", [P, O2, 2]), asb("rs1", [P, O2])
        sc1, sh1 = asb("sc1", [P, O2]), asb("sh1", [P, O2])
        mv2, rs2, sc2, sh2 = asb("mv2", [P, 1, 2]), asb("rs2", [P, 1]), asb("sc2", [P, 1]), asb("sh2", [P, 1])
        w_all = asb("w_all", [P, T, N])
        RK = asb("RK", [P, T, P])
        pT = asb("pT", [P, N])
        hT, Vn, Tb = asb("hT", [P, N]), asb("Vn", [P, T, P]), asb("Tb", [P, N])
        Sc = asb("Sc", [P, T])
        nmax, rsum, rinv, rok = asb("nmax", [P, 1]), asb("rsum", [P, 1]), asb("rinv", [P, 1]), asb("rok", [P, 1])
        si = asb("si", [P, 1])
        ah = asb("ah", [P, 4, P])
        neg_o, exp_o, pos_o = asb("neg_o", [P, P]), asb("exp_o", [P, P]), asb("pos_o", [P, P])

        x_loaded, var_ready, rstd_ready, h_ready = (asem(n) for n in ("x_loaded", "var_ready", "rstd_ready", "h_ready"))
        adj_loaded, adj_real, adjT_made = (asem(n) for n in ("adj_loaded", "adj_real", "adjT_made"))
        logits_ready, exp_ready, w_ready, w_saved = (asem(n) for n in ("logits_ready", "exp_ready", "w_ready", "w_saved"))
        wT_made, wT_ready, whT_made, whT_ready = (asem(n) for n in ("wT_made", "wT_ready", "whT_made", "whT_ready"))
        y_made, y_ready, y_saved = (asem(n) for n in ("y_made", "y_ready", "y_saved"))

        def any_norm_dve(dve, count):
            for t in range(T):
                nc.vector.bn_stats(lstat[:, t, :], xg[:, t, :])
            dve.drain()
            for t in range(T):
                nc.vector.bn_aggr(lmv[:, t, :], lstat[:, t, :])
            dve.drain()
            nc.vector.tensor_scalar(lrs[:, :], lmv[:, :, 1], LN_EPS, None, ALU.add).then_inc(var_ready, 1)
            dve.wait_ge(rstd_ready, count)
            for t in range(T):
                nc.vector.tensor_scalar(cen[:, t, :], xg[:, t, :], lmv[:, t, 0:1], lrs[:, t:t + 1], ALU.subtract, ALU.mult)
            dve.drain()
            nc.vector.tensor_scalar(hg[:, :, :], cen[:, :, :], 0.0, None, ALU.max).then_inc(h_ready, 1)

        with nc.allow_non_contiguous_dma("column blocks of adj"), nc.Block() as block:
            @block.sync
            def _(sp):
                with sp.Fori(0, B) as b:
                    sp.wait_ge(y_saved, b * T * 16 + 16)
                    sp.dma_start(xg[:, :, :], x_v[b]).then_inc(x_loaded, 16)
                    with sp.Fori(0, T) as t:
                        n = b * T + t
                        sp.wait_ge(y_saved, n * 16 + 16)
                        sp.dma_start(adj_i[:, :].rearrange("p (t c) -> p t c", t=T),
                                     adj_cols[b, :, :, bass.ts(t, P)]).then_inc(adj_loaded, 16)
                        sp.wait_ge(w_ready, n + 1)
                        sp.dma_start(w_dram[b, bass.ts(t, P), :], pro[:, :]).then_inc(w_saved, 16)
                        sp.wait_ge(w_saved, n * 16 + 16)
                        sp.wait_ge(y_ready, n + 1)
                        sp.dma_start(y_dram[b, t], yT[:, :, :]).then_inc(y_saved, 16)
                sp.wait_ge(y_saved, B * T * 16 + 16)

            @block.gpsimd
            def _(pool):
                pool.memset(nmax[:, :], 0.0).then_inc(y_saved, 16)
                with pool.Fori(0, B) as b:
                    pool.wait_ge(var_ready, b + 1)
                    pool.tensor_tensor(lrs[:, :], lrs[:, :], mhalf[:, :], ALU.pow).then_inc(rstd_ready, 1)

            @block.vector
            def _(dve):
                with dve.Fori(0, B) as b:
                    dve.wait_ge(x_loaded, b * 16 + 16)
                    any_norm_dve(dve, b + 1)
                    with dve.Fori(0, T) as t:
                        n = b * T + t
                        dve.wait_ge(adj_loaded, n * 16 + 16)
                        nc.vector.tensor_copy(tmp[:, :], adj_i[:, :]).then_inc(adj_real, 1)
                        dve.wait_ge(adjT_made, n + 1)
                        nc.vector.tensor_copy(val[:, :], pair(0))
                        dve.drain()
                        nc.vector.tensor_scalar(msk[:, :], val[:, :], 0.0, None, ALU.not_equal)
                        dve.drain()
                        nc.vector.tensor_scalar(sco[:, :], msk[:, :], 1.0, NEG_SOFT, ALU.subtract, ALU.mult)
                        dve.drain()
                        nc.vector.tensor_tensor(sco[:, :], sco[:, :], val[:, :], ALU.add)
                        dve.drain()
                        nc.vector.reduce_max(nmax[:, :], sco[:, :], AXX, negate=True).then_inc(logits_ready, 1)
                        dve.wait_ge(exp_ready, n + 1)
                        nc.vector.reciprocal(rinv[:, :], rsum[:, :])
                        dve.drain()
                        nc.vector.scalar_tensor_tensor(pro[:, :], pro[:, :], rinv[:, 0:1], msk[:, :],
                                                       ALU.mult, ALU.mult).then_inc(w_ready, 1)
                        dve.wait_ge(y_made, n + 1)
                        for o in range(O2):
                            nc.vector.tensor_scalar(yT[:, o, :], ps[:, 5, o * P:o * P + P], b1_sb[:, o:o + 1], None, ALU.add)
                        dve.drain()
                        for o in range(O2):
                            last = nc.vector.bn_stats(stats1[:, o, bass.ds(n, 1), :].rearrange("p a s -> p (a s)"),
                                                      yT[:, o, :])
                        last.then_inc(y_ready, 1)

            @block.scalar
            def _(act):
                with act.Fori(0, B) as b:
                    with act.Fori(0, T) as t:
                        n = b * T + t
                        act.wait_ge(logits_ready, n + 1)
                        nc.scalar.activation(pro[:, :], sco[:, :], ACT.Exp, bias=nmax[:, 0:1],
                                             accum_out=rsum[:, 0:1]).then_inc(exp_ready, 1)
                        act.wait_ge(wT_made, n + 1)
                        nc.scalar.copy(proT[:, :, :].rearrange("p t c -> p (t c)"), pair(1)).then_inc(wT_ready, 1)
                        act.wait_ge(whT_made, n + 1)
                        nc.scalar.copy(whT[:, :], ps[:, 4, 0:P]).then_inc(whT_ready, 1)

            @block.tensor
            def _(pe):
                with pe.Fori(0, B) as b:
                    with pe.Fori(0, T) as t:
                        n = b * T + t
                        pe.wait_ge(adj_real, n + 1)
                        for r in range(T):
                            last = nc.tensor.transpose(pair(0)[:, r * P:r * P + P], tmp[:, r * P:r * P + P], ident[:, :])
                        last.then_inc(adjT_made, 1)
                        pe.wait_ge(w_ready, n + 1)
                        for r in range(T):
                            last = nc.tensor.transpose(pair(1)[:, r * P:r * P + P], pro[:, r * P:r * P + P], ident[:, :])
                        last.then_inc(wT_made, 1)
                        pe.wait_ge(wT_ready, n + 1)
                        for r in range(T):
                            last = nc.tensor.matmul(ps[:, 4, 0:P], hg[:, r, :], proT[:, r, :], start=(r == 0), stop=(r == T - 1))
                        last.then_inc(whT_made, 1)
                        pe.wait_ge(whT_ready, n + 1)
                        for o in range(O2):
                            last = nc.tensor.matmul(ps[:, 5, o * P:o * P + P], k1_sb[:, o * P:o * P + P], whT[:, :],
                                                    start=True, stop=True)
                        last.then_inc(y_made, 1)

        var1, rstd1, w_in, y_in, yn_ready = (asem(n) for n in ("var1", "rstd1", "w_in", "y_in", "yn_ready"))
        rk_made, rk_ready, pT_made, pT_ready, pT_saved = (asem(n) for n in ("rk_made", "rk_ready", "pT_made", "pT_ready", "pT_saved"))

        with nc.Block() as block:
            @block.sync
            def _(sp):
                with sp.Fori(0, B) as b:
                    sp.wait_ge(pT_saved, b * 16 + 16)
                    sp.dma_start(w_all[:, :, :], w_dram[b].rearrange("(t p) r -> p t r", p=P)).then_inc(w_in, 16)
                    with sp.Fori(0, T) as t:
                        sp.wait_ge(rk_made, b * T + t + 1)
                        sp.dma_start(yT[:, :, :], y_dram[b, t]).then_inc(y_in, 16)
                    sp.wait_ge(pT_ready, b + 1)
                    sp.dma_start(pT_dram[b], pT[:, :]).then_inc(pT_saved, 16)
                sp.wait_ge(pT_saved, B * 16 + 16)

            @block.gpsimd
            def _(pool):
                pool.memset(nmax[:, :], 0.0).then_inc(pT_saved, 16)
                pool.memset(rsum[:, :], 0.0).then_inc(rk_made, 1)
                pool.wait_ge(var1, 1)
                pool.tensor_tensor(rs1[:, :], rs1[:, :], mhalf[:, 0:O2], ALU.pow).then_inc(rstd1, 1)

            @block.vector
            def _(dve):
                for o in range(O2):
                    nc.vector.bn_aggr(mv1[:, o, :], stats1[:, o, :, :].rearrange("p n s -> p (n s)"))
                dve.drain()
                nc.vector.tensor_scalar(rs1[:, :], mv1[:, :, 1], BN_EPS, None, ALU.add).then_inc(var1, 1)
                dve.wait_ge(rstd1, 1)
                nc.vector.tensor_tensor(sc1[:, :], rs1[:, :], g1_sb[:, :], ALU.mult)
                with dve.Fori(0, B) as b:
                    with dve.Fori(0, T) as t:
                        n = b * T + t
                        dve.drain()
                        dve.wait_ge(y_in, n * 16 + 16)
                        for o in range(O2):
                            nc.vector.tensor_scalar(yn[:, o, :], yT[:, o, :], mv1[:, o, 0:1], sc1[:, o:o + 1],
                                                    ALU.subtract, ALU.mult)
                        dve.drain()
                        for o in range(O2):
                            last = nc.vector.tensor_scalar(yn[:, o, :], yn[:, o, :], be1_sb[:, o:o + 1], None, ALU.add)
                        last.then_inc(yn_ready, 1)
                        dve.wait_ge(rk_made, n + 2)
                    dve.wait_ge(pT_made, b + 1)
                    nc.vector.tensor_scalar(pT[:, :], pair(1), b2_sb[:, 0:1], None, ALU.add)
                    dve.drain()
                    for c in range(CH):
                        last = nc.vector.bn_stats(stats2[:, bass.ds(b * CH + c, 1), :].rearrange("p a s -> p (a s)"),
                                                  pT[:, c * HALF:(c + 1) * HALF])
                    last.then_inc(pT_ready, 1)
                    dve.wait_ge(pT_saved, b * 16 + 32)

            @block.scalar
            def _(act):
                with act.Fori(0, B) as b:
                    with act.Fori(0, T) as t:
                        n = b * T + t
                        act.wait_ge(rk_made, n + 2)
                        nc.scalar.copy(RK[:, bass.ds(t, 1), :].rearrange("p a d -> p (a d)"), ps[:, 0, 0:P]).then_inc(rk_ready, 1)

            @block.tensor
            def _(pe):
                with pe.Fori(0, B) as b:
                    with pe.Fori(0, T) as t:
                        n = b * T + t
                        pe.wait_ge(yn_ready, n + 1)
                        for o in range(O2):
                            last = nc.tensor.matmul(ps[:, 0, 0:P], yn[:, o, :], k2_sb[:, o, :], start=(o == 0), stop=(o == O2 - 1))
                        last.then_inc(rk_made, 1)
                        pe.wait_ge(rk_ready, n + 1)
                    pe.wait_ge(w_in, b * 16 + 16)
                    for c in range(CH):
                        for t in range(T):
                            last = nc.tensor.matmul(ps[:, 2 + c, :], RK[:, t, :], w_all[:, t, c * HALF:(c + 1) * HALF],
                                                    start=(t == 0), stop=(t == T - 1))
                    last.then_inc(pT_made, 1)

        (var2, rstd2, g_loaded, q_ready, qT_made, var3, rstd3, hn_ready, hT_made, hT_ready, proj_made, V_ready,
         row_loaded, row_real, score_made, score_ready, score_used, lg_ready, ex_ready, at_ready, atT_made, atT_ready,
         o_made, neg_ready, elu_exp, tile_done, x_saved, ah_ready) = (asem(n) for n in (
            "var2", "rstd2", "g_loaded", "q_ready", "qT_made", "var3", "rstd3", "hn_ready", "hT_made", "hT_ready", "proj_made",
            "V_ready", "row_loaded", "row_real", "score_made", "score_ready", "score_used", "lg_ready", "ex_ready",
            "at_ready", "atT_made", "atT_ready", "o_made", "neg_ready", "elu_exp", "tile_done", "x_saved", "ah_ready"))
        LAYERS = 3

        with nc.Block() as block:
            @block.sync
            def _(sp):
                with sp.Fori(0, B) as b:
                    sp.wait_ge(x_saved, b * 16 + 16)
                    sp.dma_start(xg[:, :, :], x_v[b]).then_inc(g_loaded, 16)
                    sp.dma_start(pT[:, :], pT_dram[b]).then_inc(g_loaded, 16)
                    for layer in range(LAYERS):
                        with sp.Fori(0, T) as t:
                            n = (b * LAYERS + layer) * T + t
                            sp.wait_ge(tile_done, n + 1)
                            sp.dma_start(adj_i[:, :], adj[b, bass.ts(t, P), :]).then_inc(row_loaded, 16)
                    sp.wait_ge(tile_done, (b + 1) * LAYERS * T + 1)
                    sp.dma_start(out_v[b], xg[:, :, :]).then_inc(x_saved, 16)
                sp.wait_ge(x_saved, B * 16 + 16)

            @block.gpsimd
            def _(pool):
                pool.memset(si[:, :], 0.0).then_inc(x_saved, 16)
                pool.memset(rok[:, :], 0.0).then_inc(tile_done, 1)
                pool.wait_ge(var2, 1)
                pool.tensor_tensor(rs2[:, :], rs2[:, :], mhalf[:, 0:1], ALU.pow).then_inc(rstd2, 1)
                with pool.Fori(0, B * LAYERS) as m:
                    pool.wait_ge(var3, m + 1)
                    pool.tensor_tensor(lrs[:, :], lrs[:, :], mhalf[:, :], ALU.pow).then_inc(rstd3, 1)

            def norm_dve(dve, count):
                for t in range(T):
                    nc.vector.bn_stats(lstat[:, t, :], xg[:, t, :])
                dve.drain()
                for t in range(T):
                    nc.vector.bn_aggr(lmv[:, t, :], lstat[:, t, :])
                dve.drain()
                nc.vector.tensor_scalar(lrs[:, :], lmv[:, :, 1], LN_EPS, None, ALU.add).then_inc(var3, 1)
                dve.wait_ge(rstd3, count)
                for t in range(T):
                    nc.vector.tensor_scalar(cen[:, t, :], xg[:, t, :], lmv[:, t, 0:1], lrs[:, t:t + 1],
                                            ALU.subtract, ALU.mult)
                dve.drain()
                nc.vector.tensor_scalar(hg[:, :, :], cen[:, :, :], 0.0, None, ALU.max).then_inc(hn_ready, 1)

            @block.vector
            def _(dve):
                nc.vector.bn_aggr(mv2[:, 0, :], stats2[:, :, :].rearrange("p n s -> p (n s)"))
                dve.drain()
                nc.vector.tensor_scalar(rs2[:, :], mv2[:, :, 1], BN_EPS, None, ALU.add).then_inc(var2, 1)
                dve.wait_ge(rstd2, 1)
                nc.vector.tensor_tensor(sc2[:, :], rs2[:, :], g2_sb[:, :], ALU.mult)
                with dve.Fori(0, B) as b:
                    dve.drain()
                    dve.wait_ge(g_loaded, b * 32 + 32)
                    nc.vector.tensor_scalar(pT[:, :], pT[:, :], mv2[:, 0, 0:1], sc2[:, 0:1], ALU.subtract, ALU.mult)
                    dve.drain()
                    nc.vector.tensor_scalar(pT[:, :], pT[:, :], be2_sb[:, 0:1], None, ALU.add).then_inc(q_ready, 1)
                    dve.wait_ge(qT_made, b + 1)
                    nc.vector.tensor_tensor(xg[:, :, :], xg[:, :, :], pair(0).rearrange("p (t d) -> p t d", t=T), ALU.add)
                    for layer in range(LAYERS):
                        m = b * LAYERS + layer
                        dve.drain()
                        norm_dve(dve, m + 1)
                        dve.wait_ge(V_ready, m + 1)
                        nc.vector.memset(rok[:, :], 1.0)
                        with dve.Fori(0, T) as t:
                            n = m * T + t
                            dve.wait_ge(row_loaded, n * 16 + 16)
                            nc.vector.tensor_copy(val[:, :], adj_i[:, :])
                            if layer == 1:
                                dve.memset(sco[:, :], 0.0)
                                nc.vector.memset(msk[:, :], 0.0)
                                nc.vector.tensor_copy(si[:, :], Sc[:, bass.ds(t, 1)]).then_inc(row_real, 1)
                                for k in range(4):
                                    dve.wait_ge(score_ready, (b * T + t) * 4 + k + 1)
                                    nc.vector.scalar_tensor_tensor(tmp[:, :], pro[:, :], SLOPE, pro[:, :],
                                                                   ALU.mult, ALU.max)
                                    dve.drain()
                                    nc.vector.scalar_tensor_tensor(tmp[:, :], val[:, :], float(k + 1), tmp[:, :],
                                                                   ALU.is_equal, ALU.mult)
                                    nc.vector.scalar_tensor_tensor(msk[:, :], val[:, :], float(k + 1), msk[:, :],
                                                                   ALU.is_equal, ALU.add)
                                    dve.drain()
                                    nc.vector.tensor_tensor(sco[:, :], sco[:, :], tmp[:, :], ALU.add).then_inc(score_used, 1)
                            else:
                                nc.vector.tensor_copy(si[:, :], Sc[:, bass.ds(t, 1)])
                                dve.drain()
                                nc.vector.tensor_scalar(tmp[:, :], Tb[:, :], si[:, 0:1], None, ALU.add)
                                nc.vector.tensor_scalar(msk[:, :], val[:, :], 0.0, None,
                                                        ALU.not_equal if layer == 0 else ALU.is_gt)
                                dve.drain()
                                nc.vector.scalar_tensor_tensor(sco[:, :], tmp[:, :], SLOPE, tmp[:, :], ALU.mult, ALU.max)
                                dve.drain()
                                nc.vector.tensor_tensor(sco[:, :], sco[:, :], msk[:, :], ALU.mult)
                            dve.drain()
                            nc.vector.tensor_scalar(tmp[:, :], msk[:, :], 1.0, NEG_BIG, ALU.subtract, ALU.mult)
                            dve.drain()
                            nc.vector.tensor_tensor(sco[:, :], sco[:, :], tmp[:, :], ALU.add)
                            dve.drain()
                            nc.vector.reduce_max(nmax[:, :], sco[:, :], AXX, negate=True).then_inc(lg_ready, 1)
                            dve.wait_ge(ex_ready, n + 1)
                            nc.vector.reciprocal(rinv[:, :], rsum[:, :])
                            if layer == 0:
                                nc.vector.tensor_scalar(rok[:, :], nmax[:, :], NEG_BIG / 2, None, ALU.is_lt)
                                dve.drain()
                                nc.vector.tensor_tensor(rinv[:, :], rinv[:, :], rok[:, :], ALU.mult)
                            dve.drain()
                            nc.vector.tensor_scalar(pro[:, :], pro[:, :], rinv[:, 0:1], None, ALU.mult).then_inc(at_ready, 1)
                            dve.wait_ge(o_made, n + 1)
                            xt = xg[:, bass.ds(t, 1), :].rearrange("p a d -> p (a d)")
                            if layer < 2:
                                nc.vector.tensor_copy(pos_o[:, :], ps[:, 2, 0:P])
                                dve.drain()
                            else:
                                nc.vector.tensor_scalar(neg_o[:, :], ps[:, 2, 0:P], 0.0, None, ALU.min)
                                nc.vector.tensor_scalar(pos_o[:, :], ps[:, 2, 0:P], 0.0, None, ALU.max).then_inc(neg_ready, 1)
                                dve.drain()
                                dve.wait_ge(elu_exp, b * T + t + 1)
                                nc.vector.scalar_tensor_tensor(pos_o[:, :], exp_o[:, :], -1.0, pos_o[:, :], ALU.add, ALU.add)
                                dve.drain()
                            nc.vector.tensor_tensor(xt, xt, pos_o[:, :], ALU.add).then_inc(tile_done, 1)

            @block.scalar
            def _(act):
                with act.Fori(0, B) as b:
                    for layer in range(LAYERS):
                        m = b * LAYERS + layer
                        act.wait_ge(hT_made, m + 1)
                        nc.scalar.copy(hT[:, :], pair(0)).then_inc(hT_ready, 1)
                        act.wait_ge(proj_made, m + 1)
                        if layer == 1:
                            nc.scalar.copy(Sc[:, :], mhalf[:, :])
                            nc.scalar.copy(Vn[:, :, :], hg[:, :, :]).then_inc(V_ready, 1)
                        else:
                            nc.scalar.copy(Tb[:, :], pair(2))
                            nc.scalar.copy(Sc[:, :], ps[:, 6, 0:T])
                            nc.scalar.copy(Vn[:, :, :].rearrange("p t d -> p (t d)"), pair(1)).then_inc(V_ready, 1)
                        with act.Fori(0, T) as t:
                            n = m * T + t
                            if layer == 1:
                                act.wait_ge(row_real, b * T + t + 1)
                                for k in range(4):
                                    last = nc.scalar.mul(ah[:, k, :], hT[:, bass.ts(t, P)], a2_sb[:, k:k + 1])
                                last.then_inc(ah_ready, 1)
                                for k in range(4):
                                    act.wait_ge(score_made, (b * T + t) * 4 + k + 1)
                                    if k:
                                        act.wait_ge(score_used, (b * T + t) * 4 + k)
                                    nc.scalar.copy(pro[:, :], pair(k)).then_inc(score_ready, 1)
                            act.wait_ge(lg_ready, n + 1)
                            nc.scalar.activation(pro[:, :], sco[:, :], ACT.Exp, bias=nmax[:, 0:1],
                                                 accum_out=rsum[:, 0:1]).then_inc(ex_ready, 1)
                            act.wait_ge(atT_made, n + 1)
                            nc.scalar.copy(proT[:, :, :].rearrange("p t c -> p (t c)"), pair(0)).then_inc(atT_ready, 1)
                            if layer == 2:
                                act.wait_ge(neg_ready, b * T + t + 1)
                                nc.scalar.activation(exp_o[:, :], neg_o[:, :], ACT.Exp).then_inc(elu_exp, 1)

            @block.tensor
            def _(pe):
                with pe.Fori(0, B) as b:
                    pe.wait_ge(q_ready, b + 1)
                    for t in range(T):
                        last = nc.tensor.transpose(pair(0)[:, t * P:t * P + P], pT[:, t * P:t * P + P], ident[:, :])
                    last.then_inc(qT_made, 1)
                    for layer in range(LAYERS):
                        m = b * LAYERS + layer
                        pe.wait_ge(hn_ready, m + 1)
                        for t in range(T):
                            last = nc.tensor.transpose(pair(0)[:, t * P:t * P + P], hg[:, t, :], ident[:, :])
                        last.then_inc(hT_made, 1)
                        pe.wait_ge(hT_ready, m + 1)
                        if layer != 1:
                            w = w1T if layer == 0 else w3_sb
                            v = 0 if layer == 0 else 2
                            for t in range(T):
                                nc.tensor.matmul(pair(1)[:, t * P:t * P + P], hT[:, t * P:t * P + P], w[:, :], start=True, stop=True)
                                nc.tensor.matmul(ps[:, 6, t:t + 1], hT[:, t * P:t * P + P], v_rep[:, v, 0:1], start=True, stop=True)
                            for c in range(CH):
                                nc.tensor.matmul(ps[:, 4 + c, :], v_rep[:, v + 1, :], hT[:, c * HALF:(c + 1) * HALF],
                                                 start=True, stop=True)
                        nc.tensor.matmul(ps[:, 7, 0:1], ones[:, :], ones[:, 0:1], start=True, stop=True).then_inc(proj_made, 1)
                        with pe.Fori(0, T) as t:
                            n = m * T + t
                            if layer == 1:
                                pe.wait_ge(ah_ready, b * T + t + 1)
                                for k in range(4):
                                    for c in range(CH):
                                        last = nc.tensor.matmul(ps[:, 2 * k + c, :], ah[:, k, :], hT[:, c * HALF:(c + 1) * HALF],
                                                                start=True, stop=True)
                                    last.then_inc(score_made, 1)
                            pe.wait_ge(at_ready, n + 1)
                            for r in range(T):
                                last = nc.tensor.transpose(pair(0)[:, r * P:r * P + P], pro[:, r * P:r * P + P], ident[:, :])
                            last.then_inc(atT_made, 1)
                            pe.wait_ge(atT_ready, n + 1)
                            for r in range(T):
                                last = nc.tensor.matmul(ps[:, 2, 0:P], proT[:, r, :], Vn[:, r, :], start=(r == 0), stop=(r == T - 1))
                            last.then_inc(o_made, 1)


_INS = ['x', 'adj', 'L0_gnn_kernel_1', 'L0_gnn_bias_1', 'L0_gnn_gamma_1', 'L0_gnn_beta_1', 'L0_gnn_kernel_2',
        'L0_gnn_bias_2', 'L0_gnn_gamma_2', 'L0_gnn_beta_2', 'L1_gnn_W', 'L1_gnn_a', 'L2_gnn_a_0', 'L2_gnn_a_1',
        'L2_gnn_a_2', 'L2_gnn_a_3', 'L3_gnn_W', 'L3_gnn_a']


def kernel(**inputs):
    import numpy as _np
    import concourse.bacc as _bacc
    from concourse import mybir as _mybir
    from concourse.bass_utils import run_bass_kernel_spmd as _run

    nc = _bacc.Bacc("TRN2", target_bir_lowering=False, num_devices=1)
    arrays, args = {}, []
    for name in _INS:
        a = _np.ascontiguousarray(inputs[name])
        arrays[f"in_{name}"] = a
        args.append(nc.dram_tensor(f"in_{name}", a.shape, _mybir.dt.from_np(a.dtype), kind="ExternalInput").ap())
    args.append(nc.dram_tensor("out_0", inputs["x"].shape, _mybir.dt.float32, kind="ExternalOutput").ap())
    gnn_stack_kernel(nc, *args)
    r = _run(nc, [arrays], core_ids=[0])
    return r.results[0]["out_0"]
```

```python
import numpy as np
import concourse.bass as bass
from concourse import mybir
from contextlib import ExitStack


def gnn_stack_kernel(nc, x_in, adj, k1, b1, g1, be1, k2, b2, g2, be2,
                     w_l1, a_l1, a2_0, a2_1, a2_2, a2_3, w_l3, a_l3, out):
    fp32, i32 = mybir.dt.float32, mybir.dt.int32
    fp16, bf16, u8 = mybir.dt.float16, mybir.dt.bfloat16, mybir.dt.uint8
    ALU = mybir.AluOpType
    ACT = mybir.ActivationFunctionType
    AXX = mybir.AxisListType.X

    P = 128
    B, N, D = x_in.shape
    T = N // P
    C0 = k1.shape[1]
    O2 = C0 // P
    HALF = 512
    CH = N // HALF
    NT = B * T
    LN_EPS, BN_EPS, SLOPE = 1e-5, 1e-3, 0.2
    NEG_SOFT, NEG_BIG = 1e30, 9e15

    x_v = x_in.rearrange("b (t p) d -> b p t d", p=P)
    out_v = out.rearrange("b (t p) d -> b p t d", p=P)
    adj_cols = adj.rearrange("b (t p) c -> b p t c", p=P)

    w_dram = nc.dram_tensor("w_scratch", (B, N, N), fp32).ap()
    y_dram = nc.dram_tensor("y_scratch", (B, T, P, O2, P), fp32).ap()
    pT_dram = nc.dram_tensor("pT_scratch", (B, P, N), fp32).ap()

    ctx = ExitStack()
    with ctx:
        def sb(name, shape, dt=fp32, stack=ctx):
            return stack.enter_context(nc.sbuf_tensor(name, shape, dt))

        def sem(name, stack=ctx):
            return stack.enter_context(nc.semaphore(name))

        stage_sems = []

        def stage_sem(name):
            stage_sems.append(nc.alloc_semaphore(name))
            return stage_sems[-1]

        def retire_sems():
            nc.clear_and_free_semaphores(stage_sems)
            stage_sems.clear()
            nc.all_engine_barrier()

        ident = sb("ident", [P, P])
        ones = sb("ones", [P, P])
        k1_sb = sb("k1_sb", [P, C0])
        k2_sb = sb("k2_sb", [P, O2, P])
        b1_sb, g1_sb, be1_sb = sb("b1_sb", [P, O2]), sb("g1_sb", [P, O2]), sb("be1_sb", [P, O2])
        b2_sb, g2_sb, be2_sb = sb("b2_sb", [P, 1]), sb("g2_sb", [P, 1]), sb("be2_sb", [P, 1])
        mhalf = sb("mhalf", [P, T])
        ident_bf = sb("ident_bf", [P, P], bf16)
        k1T = sb("k1T", [P, O2, P])
        deg_all, sq_all = sb("deg_all", [P, NT]), sb("sq_all", [P, NT])
        rdeg_all = sb("rdeg_all", [P, NT])
        g_acc = sb("g_acc", [P, P + 1])
        k12, c_rep = sb("k12", [P, P]), sb("c_rep", [P, P])
        mean1, rstd_1, scale1, shift1 = (sb(n, [P, O2]) for n in ("mean1", "rstd_1", "scale1", "shift1"))
        stats_2 = sb("stats_2", [P, B * CH, 6])
        r_top = sb("r_top", [P, B])
        rec_top = sb("rec_top", [P, 3, T])
        spread = sb("spread", [P, O2])
        bound_B = sb("bound_B", [P, 1])
        norm_W = sb("norm_W", [P, 1])
        ps = ctx.enter_context(nc.psum_tensor("ps", [P, 8, HALF], fp32))

        weights_in = sem("weights_in")
        ident_zero, ident_ready = sem("ident_zero"), sem("ident_ready")
        wT_made, wT_kept, reps_made = sem("wT_made"), sem("wT_kept"), sem("reps_made")
        v_made, k1T_made = sem("v_made"), sem("k1T_made")
        store_ctx = ctx.enter_context(ExitStack())

        def pair(k):
            return ps[:, 2 * k:2 * k + 2, :].rearrange("p a b -> p (a b)")

        loads0 = [(k1_sb[:, :], k1), (k2_sb[:, :, :], k2.rearrange("(o p) d -> p o d", p=P)),
                  (b1_sb[:, :], b1.rearrange("(o p) -> p o", p=P)), (g1_sb[:, :], g1.rearrange("(o p) -> p o", p=P)),
                  (be1_sb[:, :], be1.rearrange("(o p) -> p o", p=P)),
                  (b2_sb[:, :], b2.rearrange("(p o) -> p o", o=1)), (g2_sb[:, :], g2.rearrange("(p o) -> p o", o=1)),
                  (be2_sb[:, :], be2.rearrange("(p o) -> p o", o=1))]

        with nc.allow_non_contiguous_dma("small weight vectors"), nc.Block() as block:
            @block.sync
            def _(sp):
                for dst, src in loads0:
                    sp.dma_start(dst, src).then_inc(weights_in, 16)

            @block.gpsimd
            def _(pool):
                pool.memset(ident[:, :], 0.0).then_inc(ident_zero, 1)
                pool.memset(mhalf[:, :], -0.5)
                pool.wait_ge(ident_zero, 1)
                pool.affine_select(out=ident[:, :], in_=ident[:, :], compare_op=ALU.not_equal, fill=1.0,
                                   base=0, pattern=[[-1, P]], channel_multiplier=1).then_inc(ident_ready, 1)

            @block.tensor
            def _(pe):
                pe.wait_ge(weights_in, 16 * len(loads0))
                pe.wait_ge(ident_ready, 1)
                for o in range(O2):
                    last = nc.tensor.transpose(ps[:, o, 0:P], k1_sb[:, o * P:o * P + P], ident[:, :])
                last.then_inc(k1T_made, 1)

            @block.vector
            def _(dve):
                dve.memset(ones[:, :], 1.0)
                dve.wait_ge(ident_ready, 1)
                nc.vector.tensor_copy(ident_bf[:, :], ident[:, :])
                dve.wait_ge(k1T_made, 1)
                for o in range(O2):
                    nc.vector.tensor_copy(k1T[:, o, :], ps[:, o, 0:P])

        whT_dram = nc.dram_tensor("whT_scratch", (B, P, N), fp32).ap()
        maskT_dram = nc.dram_tensor("maskT_scratch", (B, P, T, N), bf16).ap()
        pTf_dram = nc.dram_tensor("pTf_scratch", (B, P, N), fp32).ap()
        NT = B * T
        RSCALE = 1024.0
        ROW_MAX = 6e4
        X0W = 2 * P + 1
        GW = P + 1

        maskT = sb("maskT", [P, B, T, N], u8, store_ctx)

        NA = 4
        with ExitStack() as a_ctx:
            def sba(name, shape, dt=fp32):
                return sb(name, shape, dt, a_ctx)

            adj_r = sba("adj_r", [P, NA, N], i32)
            adj_b = sba("adj_b", [P, 2, T, N], bf16)
            xa = sba("xa", [P, T, P])
            x0 = sba("x0", [P, 2, T, X0W], fp16)
            whn = sba("whn", [P, T, GW])
            whT_s = sba("whT_s", [P, N])
            st_a, mv_a, rs_a = sba("st_a", [P, T, 6]), sba("mv_a", [P, T, 2]), sba("rs_a", [P, T])
            tmp_a = sba("tmp_a", [P, 2, P])
            dga, dgm, rdg = sba("dga", [P, T]), sba("dgm", [P, T]), sba("rdg", [P, T])
            a_adj_in = [stage_sem(f"a_adj_in{k}") for k in range(NA)]
            (a_x_in, a_adj_used, a_var, a_rstd, a_h, a_turned, a_kept, a_wh_made, a_deg, a_tmp,
             a_wh, a_sums_made, a_gram_kept, a_whT_kept, a_whT_out) = (stage_sem(n) for n in (
                "a_x_in", "a_adj_used", "a_var", "a_rstd", "a_h", "a_turned", "a_kept", "a_wh_made", "a_deg", "a_tmp",
                "a_wh", "a_sums_made", "a_gram_kept", "a_whT_kept", "a_whT_out"))
            psT = [ps[:, k, :].bitcast(bf16) for k in range(2)]
            psW = [ps[:, 2 + k, :] for k in range(2)]
            psG = ps[:, 4, 0:GW]
            psWT = ps[:, 6:8, :].rearrange("p a b -> p (a b)")

            with nc.Block() as block:
                @block.sync
                def _(sp):
                    def graph(b, first):
                        if not first:
                            sp.wait_ge(a_h, b)
                        sp.dma_start(xa[:, :, :], x_v[b]).then_inc(a_x_in, 16)
                        for r in range(T):
                            if not (first and r < NA):
                                sp.wait_ge(a_adj_used, b * T + r - NA + 1)
                            sp.dma_start(adj_r[:, r % NA, :], adj[b, r * P:r * P + P, :]).then_inc(a_adj_in[r % NA], 16)

                    graph(0, True)
                    with sp.Fori(1, B) as b:
                        graph(b, False)

                @block.gpsimd
                def _(pool):
                    with pool.Fori(0, B) as b:
                        pool.wait_ge(a_var, b + 1)
                        pool.tensor_tensor(rs_a[:, :], rs_a[:, :], mhalf[:, :], ALU.pow).then_inc(a_rstd, 1)

                @block.vector
                def _(dve):
                    def head(b, par, c):
                        if c == 0:
                            dve.wait_ge(a_x_in, b * 16 + 16)
                            for t in range(T):
                                nc.vector.bn_stats(st_a[:, t, :], xa[:, t, :])
                            dve.drain()
                            for t in range(T):
                                nc.vector.bn_aggr(mv_a[:, t, :], st_a[:, t, :])
                            dve.drain()
                            nc.vector.tensor_scalar(rs_a[:, :], mv_a[:, :, 1], LN_EPS, None, ALU.add).then_inc(a_var, 1)
                        if c == 3:
                            dve.wait_ge(a_rstd, b + 1)
                            for t in range(T):
                                nc.vector.tensor_scalar(xa[:, t, :], xa[:, t, :], mv_a[:, t, 0:1], rs_a[:, t:t + 1],
                                                        ALU.subtract, ALU.mult)
                        if c == 4:
                            nc.vector.tensor_scalar(xa[:, :, :], xa[:, :, :], 0.0, None, ALU.max)
                        if c == 5:
                            nc.vector.tensor_copy(x0[:, par, :, 0:P], xa[:, :, :])
                        dve.wait_ge(a_adj_in[c % NA], (b * (T // NA) + c // NA + 1) * 16)
                        nc.vector.tensor_copy(adj_b[:, par, c, :], adj_r[:, c % NA, :]).then_inc(a_adj_used, 1)
                        dve.drain()
                        if c == T - 1:
                            nc.vector.tensor_tensor(x0[:, par, :, P:2 * P], xa[:, :, :], x0[:, par, :, 0:P],
                                                    ALU.subtract).then_inc(a_h, 1)

                    def tail(b, c, first):
                        n = b * T + c
                        q = psW[c % 2]
                        dve.wait_ge(a_wh_made, n + 1)
                        nc.vector.tensor_scalar(dgm[:, c:c + 1], q[:, 2 * P:2 * P + 1], 1.0, None, ALU.max)
                        nc.vector.tensor_copy(dga[:, c:c + 1], q[:, 2 * P:2 * P + 1])
                        dve.drain()
                        nc.vector.reciprocal(rdg[:, c:c + 1], dgm[:, c:c + 1]).then_inc(a_deg, 1)
                        if c == 0 and not first:
                            dve.wait_ge(a_sums_made, b)
                        dve.wait_ge(a_tmp, n + 1)
                        nc.vector.scalar_tensor_tensor(whn[:, c, 0:P], q[:, P:2 * P], rdg[:, c:c + 1], tmp_a[:, c % 2, :],
                                                       ALU.mult, ALU.add).then_inc(a_wh, 1)
                        if c == 1 and not first:
                            nc.vector.tensor_tensor(g_acc[:, :], g_acc[:, :], psG, ALU.add).then_inc(a_gram_kept, 1)

                    def graph(b, par, first, last):
                        for c in range(T):
                            tail(b, c, first)
                            if not last:
                                head(b + 1, 1 - par, c)
                        dve.drain()
                        nc.vector.tensor_copy(rdeg_all[:, bass.ds(b * T, T)], rdg[:, :])
                        nc.vector.tensor_copy(deg_all[:, bass.ds(b * T, T)], dga[:, :])
                        dve.drain()

                    nc.vector.memset(g_acc[:, :], 0.0)
                    nc.vector.memset(whn[:, :, :], 1.0)
                    nc.vector.memset(x0[:, :, :, :], 1.0)
                    dve.drain()
                    for c in range(T):
                        head(0, 0, c)
                    graph(0, 0, True, False)
                    with dve.Fori(0, B // 2 - 1) as k:
                        graph(k * 2 + 1, 1, False, False)
                        graph(k * 2 + 2, 0, False, False)
                    graph(B - 1, 1, False, True)
                    dve.wait_ge(a_sums_made, B)
                    nc.vector.tensor_tensor(g_acc[:, :], g_acc[:, :], psG, ALU.add).then_inc(a_gram_kept, 1)

                @block.scalar
                def _(act):
                    def graph(b, first):
                        for c in range(T):
                            n = b * T + c
                            act.wait_ge(a_turned, n + 1)
                            nc.scalar.activation(maskT[:, bass.ds(b, 1), c, :].rearrange("p a r -> p (a r)"), psT[c % 2], ACT.Square,
                                                 accum_out=sq_all[:, bass.ds(n, 1)]).then_inc(a_kept, 1)
                            act.wait_ge(a_deg, n + 1)
                            nc.scalar.mul(tmp_a[:, c % 2, :], psW[c % 2][:, 0:P], rdg[:, c:c + 1]).then_inc(a_tmp, 1)
                        act.wait_ge(a_sums_made, b + 1)
                        if not first:
                            act.wait_ge(a_whT_out, b * 16)
                        nc.scalar.copy(whT_s[:, :], psWT).then_inc(a_whT_kept, 1)
                        act.wait_ge(a_whT_kept, b + 1)
                        act.dma_start(whT_dram[bass.ds(b, 1)].rearrange("a p n -> (a p) n"), whT_s[:, :]).then_inc(a_whT_out, 16)

                    graph(0, True)
                    with act.Fori(1, B) as b:
                        graph(b, False)
                    act.wait_ge(a_whT_out, B * 16)

                @block.tensor
                def _(pe):
                    def sums(b, c):
                        pe.wait_ge(a_wh, b * T + c + 1)
                        nc.tensor.matmul(psG, whn[:, c, 0:P], whn[:, c, :], start=(c == 0), stop=(c == T - 1))
                        return nc.tensor.transpose(psWT[:, c * P:c * P + P], whn[:, c, 0:P], ident[:, :])

                    def graph(b, par, first):
                        pe.wait_ge(a_h, b + 1)
                        for c in range(T):
                            n = b * T + c
                            if not (first and c < 2):
                                pe.wait_ge(a_kept, n - 1)
                            for r in range(T):
                                last = nc.tensor.transpose(psT[c % 2][:, r * P:r * P + P], adj_b[:, par, r, c * P:c * P + P],
                                                           ident_bf[:, :])
                            last.then_inc(a_turned, 1)
                            if not (first and c < 2):
                                pe.wait_ge(a_wh, n - 1)
                            for r in range(T):
                                last = nc.tensor.matmul(psW[c % 2][:, 0:X0W], adj_b[:, par, r, c * P:c * P + P], x0[:, par, r, :],
                                                        start=(r == 0), stop=(r == T - 1))
                            last.then_inc(a_wh_made, 1)
                            if c == 2 and not first:
                                pe.wait_ge(a_gram_kept, b)
                                pe.wait_ge(a_whT_kept, b)
                            if c >= 2:
                                sums(b, c - 2)
                        sums(b, T - 2)
                        sums(b, T - 1).then_inc(a_sums_made, 1)

                    graph(0, 0, True)
                    with pe.Fori(0, B // 2 - 1) as k:
                        graph(k * 2 + 1, 1, False)
                        graph(k * 2 + 2, 0, False)
                    graph(B - 1, 1, False)

        with ExitStack() as m_ctx:
            def sbm(name, shape, dt=fp32):
                return sb(name, shape, dt, m_ctx)

            eg, cov, m_row = sbm("eg", [P, GW]), sbm("cov", [P, P]), sbm("m_row", [1, P])
            z, sk2, shr = sbm("z", [P, C0]), sbm("sk2", [P, O2, P]), sbm("shr", [P, O2, P])
            var_1, inv_var = sbm("var_1", [P, O2]), sbm("inv_var", [P, O2])
            (m_eg, m_row_made, m_row_kept, m_mm, m_cov, m_u, m_z, m_var_made, m_var, m_rstd, m_scaled, m_k12) = (stage_sem(n) for n in (
                "m_eg", "m_row_made", "m_row_kept", "m_mm", "m_cov", "m_u", "m_z", "m_var_made", "m_var", "m_rstd", "m_scaled", "m_k12"))
            with nc.Block() as block:
                @block.gpsimd
                def _(pool):
                    pool.wait_ge(m_var, 1)
                    pool.tensor_tensor(rstd_1[:, :], var_1[:, :], mhalf[:, 0:O2], ALU.pow).then_inc(m_rstd, 1)

                @block.tensor
                def _(pe):
                    pe.wait_ge(m_eg, 1)
                    nc.tensor.transpose(ps[0:1, 0, 0:P], eg[:, P:GW], ident[:, :]).then_inc(m_row_made, 1)
                    pe.wait_ge(m_row_kept, 1)
                    nc.tensor.matmul(ps[:, 1, 0:P], m_row[0:1, :], m_row[0:1, :], start=True, stop=True).then_inc(m_mm, 1)
                    pe.wait_ge(m_cov, 1)
                    nc.tensor.matmul(ps[:, 2, 0:C0], cov[:, :], k1_sb[:, :], start=True, stop=True).then_inc(m_u, 1)
                    pe.wait_ge(m_z, 1)
                    for o in range(O2):
                        nc.tensor.matmul(ps[:, 3, o:o + 1], z[:, o * P:o * P + P], ones[:, 0:1], start=True, stop=True)
                        last = nc.tensor.matmul(ps[:, 3, O2 + o:O2 + o + 1], k1_sb[:, o * P:o * P + P], eg[:, P:GW],
                                                start=True, stop=True)
                    last.then_inc(m_var_made, 1)
                    pe.wait_ge(m_scaled, 1)
                    for o in range(O2):
                        nc.tensor.matmul(ps[:, 4, 0:P], k1T[:, o, :], sk2[:, o, :], start=(o == 0), stop=(o == O2 - 1))
                    for o in range(O2):
                        last = nc.tensor.matmul(ps[:, 5, 0:P], shr[:, o, :], k2_sb[:, o, :], start=(o == 0), stop=(o == O2 - 1))
                    last.then_inc(m_k12, 1)

                @block.vector
                def _(dve):
                    nc.vector.tensor_scalar(eg[:, :], g_acc[:, :], 1.0 / (B * N), None, ALU.mult).then_inc(m_eg, 1)
                    dve.wait_ge(m_row_made, 1)
                    nc.vector.tensor_copy(m_row[:, :], ps[0:1, 0, 0:P]).then_inc(m_row_kept, 1)
                    dve.wait_ge(m_mm, 1)
                    nc.vector.tensor_tensor(cov[:, :], eg[:, 0:P], ps[:, 1, 0:P], ALU.subtract).then_inc(m_cov, 1)
                    dve.wait_ge(m_u, 1)
                    nc.vector.tensor_tensor(z[:, :], k1_sb[:, :], ps[:, 2, 0:C0], ALU.mult).then_inc(m_z, 1)
                    dve.wait_ge(m_var_made, 1)
                    nc.vector.tensor_scalar(var_1[:, :], ps[:, 3, 0:O2], 0.0, BN_EPS, ALU.max, ALU.add).then_inc(m_var, 1)
                    nc.vector.tensor_copy(spread[:, :], ps[:, 3, O2:2 * O2])
                    dve.drain()
                    nc.vector.tensor_tensor(spread[:, :], spread[:, :], spread[:, :], ALU.mult)
                    nc.vector.reciprocal(inv_var[:, :], var_1[:, :])
                    dve.drain()
                    nc.vector.tensor_tensor(spread[:, :], spread[:, :], inv_var[:, :], ALU.mult)
                    nc.vector.tensor_tensor(mean1[:, :], b1_sb[:, :], ps[:, 3, O2:2 * O2], ALU.add)
                    dve.drain()
                    nc.vector.tensor_tensor(shift1[:, :], b1_sb[:, :], mean1[:, :], ALU.subtract)
                    dve.wait_ge(m_rstd, 1)
                    nc.vector.tensor_tensor(scale1[:, :], rstd_1[:, :], g1_sb[:, :], ALU.mult)
                    dve.drain()
                    nc.vector.tensor_tensor(shift1[:, :], shift1[:, :], scale1[:, :], ALU.mult)
                    dve.drain()
                    nc.vector.tensor_tensor(shift1[:, :], shift1[:, :], be1_sb[:, :], ALU.add)
                    dve.drain()
                    for o in range(O2):
                        nc.vector.tensor_scalar(sk2[:, o, :], k2_sb[:, o, :], scale1[:, o:o + 1], None, ALU.mult)
                        last = nc.vector.tensor_scalar(shr[:, o, :], ones[:, :], shift1[:, o:o + 1], None, ALU.mult)
                    last.then_inc(m_scaled, 1)
                    dve.wait_ge(m_k12, 1)
                    nc.vector.tensor_copy(k12[:, :], ps[:, 4, 0:P])
                    nc.vector.tensor_copy(c_rep[:, :], ps[:, 5, 0:P])

        with ExitStack() as b_ctx:
            def sbb(name, shape, dt=fp32):
                return sb(name, shape, dt, b_ctx)

            whT_b = sbb("whT_b", [P, 2, N])
            mask_b = sbb("mask_b", [P, 2, T, N], bf16)
            row = sbb("row", [P, T, P])
            rdg_b = sbb("rdg_b", [P, T])
            row_hi, row_lo = sbb("row_hi", [P, 2, T, P], fp16), sbb("row_lo", [P, 2, T, P], fp16)
            pT_b = sbb("pT_b", [P, 2, N])
            b_whT_in = [stage_sem(f"b_whT_in{k}") for k in range(2)]
            b_mask_out = [stage_sem(f"b_mask_out{k}") for k in range(2)]
            b_pT_out = [stage_sem(f"b_pT_out{k}") for k in range(2)]
            (b_row_made, b_row, b_hi, b_lo, b_mask, b_p_made, b_pT, b_stats) = (stage_sem(n) for n in (
                "b_row_made", "b_row", "b_hi", "b_lo", "b_mask", "b_p_made", "b_pT", "b_stats"))
            psR = ps[:, 0:2, :].rearrange("p a b -> p (a b)")
            psP = [ps[:, 2 + 2 * k:4 + 2 * k, :].rearrange("p a b -> p (a b)") for k in range(2)]
            MC = 4
            TC = T // MC

            with nc.Block() as block:
                @block.sync
                def _(sp):
                    def load(b, par, fresh):
                        if not fresh:
                            sp.wait_ge(b_row_made, b - 1)
                        sp.dma_start(whT_b[:, par, :], whT_dram[bass.ds(b, 1)].rearrange("a p n -> (a p) n")).then_inc(b_whT_in[par], 16)

                    def save(b, par):
                        sp.wait_ge(b_mask, (b + 1) * MC)
                        sp.dma_start(maskT_dram[bass.ds(b, 1)].rearrange("a p t n -> (a p) t n"), mask_b[:, par, :, :]).then_inc(b_mask_out[par], 16)
                        sp.wait_ge(b_pT, b + 1)
                        sp.dma_start(pTf_dram[bass.ds(b, 1)].rearrange("a p n -> (a p) n"), pT_b[:, par, :]).then_inc(b_pT_out[par], 16)

                    load(0, 0, True)
                    load(1, 1, True)
                    with sp.Fori(0, B // 2 - 1) as k:
                        for par in range(2):
                            load(k * 2 + 2 + par, par, False)
                            save(k * 2 + par, par)
                    for par in range(2):
                        save(B - 2 + par, par)
                    for par in range(2):
                        sp.wait_ge(b_mask_out[par], B // 2 * 16)
                        sp.wait_ge(b_pT_out[par], B // 2 * 16)

                @block.vector
                def _(dve):
                    def graph(b, par, fresh):
                        dve.drain()
                        nc.vector.tensor_copy(rdg_b[:, :], rdeg_all[:, bass.ds(b * T, T)])
                        dve.wait_ge(b_row_made, b + 1)
                        nc.vector.tensor_tensor(row[:, :, :], psR.rearrange("p (t d) -> p t d", t=T),
                                                c_rep[:, :].unsqueeze(1).to_broadcast([P, T, P]), ALU.add)
                        dve.drain()
                        nc.vector.tensor_scalar(rdg_b[:, :], rdg_b[:, :], RSCALE, None, ALU.mult)
                        dve.drain()
                        nc.vector.tensor_tensor(row[:, :, :], row[:, :, :],
                                                rdg_b[:, :].unsqueeze(2).to_broadcast([P, T, P]), ALU.mult)
                        dve.drain()
                        nc.vector.tensor_reduce(r_top[:, bass.ds(b, 1)], row[:, :, :].rearrange("p t d -> p (t d)"), AXX, ALU.max,
                                                apply_absolute_value=True)
                        dve.drain()
                        nc.vector.tensor_scalar(row[:, :, :], row[:, :, :], ROW_MAX, -ROW_MAX, ALU.min, ALU.max).then_inc(b_row, 1)
                        dve.wait_ge(b_hi, b + 1)
                        nc.vector.tensor_tensor(row_lo[:, par, :, :], row[:, :, :], row_hi[:, par, :, :], ALU.subtract).then_inc(b_lo, 1)

                    def stats(b, par):
                        dve.wait_ge(b_pT, b + 1)
                        for c in range(CH):
                            last = nc.vector.bn_stats(stats_2[:, bass.ds(b * CH + c, 1), :].rearrange("p a s -> p (a s)"),
                                                      pT_b[:, par, c * HALF:(c + 1) * HALF])
                        last.then_inc(b_stats, 1)

                    graph(0, 0, True)
                    graph(1, 1, True)
                    with dve.Fori(0, B // 2 - 1) as k:
                        for par in range(2):
                            stats(k * 2 + par, par)
                            graph(k * 2 + 2 + par, par, False)
                    for par in range(2):
                        stats(B - 2 + par, par)

                @block.scalar
                def _(act):
                    def widen(b, par, m):
                        nc.scalar.copy(mask_b[:, par, m * TC:(m + 1) * TC, :],
                                       maskT[:, bass.ds(b, 1), m * TC:(m + 1) * TC, :].rearrange("p a t n -> p (a t) n")).then_inc(b_mask, 1)

                    def graph(b, par, k, fresh):
                        if not fresh:
                            act.wait_ge(b_mask_out[par], k * 16)
                            act.wait_ge(b_p_made, b - 1)
                        for m in range(MC // 2):
                            widen(b, par, m)
                        act.wait_ge(b_row, b + 1)
                        nc.scalar.copy(row_hi[:, par, :, :], row[:, :, :]).then_inc(b_hi, 1)
                        for m in range(MC // 2, MC):
                            widen(b, par, m)

                    def people(b, par, k, fresh):
                        act.wait_ge(b_p_made, b + 1)
                        if not fresh:
                            act.wait_ge(b_pT_out[par], k * 16)
                            act.wait_ge(b_stats, b - 1)
                        nc.scalar.activation(pT_b[:, par, :], psP[par], ACT.Identity, bias=b2_sb[:, 0:1],
                                             scale=1.0 / RSCALE).then_inc(b_pT, 1)

                    graph(0, 0, 0, True)
                    graph(1, 1, 0, True)
                    people(0, 0, 0, True)
                    graph(2, 0, 1, False)
                    people(1, 1, 0, True)
                    graph(3, 1, 1, False)
                    with act.Fori(1, B // 2 - 1) as k:
                        for par in range(2):
                            people(k * 2 + par, par, k, False)
                            graph(k * 2 + 2 + par, par, k + 1, False)
                    for par in range(2):
                        people(B - 2 + par, par, B // 2 - 1, False)

                @block.tensor
                def _(pe):
                    def rows(b, par, k, fresh):
                        pe.wait_ge(b_whT_in[par], (k + 1) * 16)
                        if not fresh:
                            pe.wait_ge(b_row, b)
                        for t in range(T):
                            last = nc.tensor.matmul(psR[:, t * P:t * P + P], whT_b[:, par, t * P:t * P + P], k12[:, :],
                                                    start=True, stop=True)
                        last.then_inc(b_row_made, 1)

                    def product(b, par, fresh):
                        pe.wait_ge(b_mask, (b + 1) * MC)
                        pe.wait_ge(b_lo, b + 1)
                        if not fresh:
                            pe.wait_ge(b_pT, b - 1)
                        for c in range(CH):
                            for t in range(T):
                                for part in (row_hi, row_lo):
                                    last = nc.tensor.matmul(psP[par][:, c * HALF:(c + 1) * HALF], part[:, par, t, :],
                                                            mask_b[:, par, t, c * HALF:(c + 1) * HALF],
                                                            start=(t == 0 and part is row_hi), stop=(t == T - 1 and part is row_lo))
                        last.then_inc(b_p_made, 1)

                    rows(0, 0, 0, True)
                    rows(1, 1, 0, False)
                    product(0, 0, True)
                    rows(2, 0, 1, False)
                    product(1, 1, True)
                    rows(3, 1, 1, False)
                    with pe.Fori(1, B // 2 - 1) as k:
                        for par in range(2):
                            product(k * 2 + par, par, False)
                            rows(k * 2 + 2 + par, par, k + 1, False)
                    for par in range(2):
                        product(B - 2 + par, par, False)
        store_ctx.close()
        retire_sems()
        w1_sb, w1T = sb("w1_sb", [P, P]), sb("w1T", [P, P])
        w3_sb, w3T = sb("w3_sb", [P, P]), sb("w3T", [P, P])
        a1_sb, a3_sb = sb("a1_sb", [P, 2]), sb("a3_sb", [P, 2])
        a2_sb = sb("a2_sb", [P, 4])
        a_rep = sb("a_rep", [P, 4, P])
        v_rep = sb("v_rep", [P, 4, P])
        loads1 = [(w1_sb[:, :], w_l1), (w3_sb[:, :], w_l3),
                  (a1_sb[:, :], a_l1.rearrange("(o p) -> p o", p=P)),
                  (a3_sb[:, :], a_l3.rearrange("(o p) k -> p (o k)", p=P))] \
            + [(a2_sb[:, k:k + 1], a) for k, a in enumerate((a2_0, a2_1, a2_2, a2_3))]
        with nc.allow_non_contiguous_dma("small weight vectors"), nc.Block() as block:
            @block.sync
            def _(sp):
                for dst, src in loads1:
                    sp.dma_start(dst, src).then_inc(weights_in, 16)

            @block.tensor
            def _(pe):
                pe.wait_ge(weights_in, 16 * (len(loads0) + len(loads1)))
                nc.tensor.transpose(ps[:, 0, 0:P], w1_sb[:, :], ident[:, :])
                nc.tensor.transpose(ps[:, 1, 0:P], w3_sb[:, :], ident[:, :]).then_inc(wT_made, 1)
                pe.wait_ge(wT_kept, 1)
                pe.wait_ge(reps_made, 1)
                nc.tensor.matmul(ps[:, 2, 0:2 * P], w1_sb[:, :], a_rep[:, 0:2, :], start=True, stop=True)
                nc.tensor.matmul(ps[:, 3, 0:2 * P], w3T[:, :], a_rep[:, 2:4, :], start=True, stop=True).then_inc(v_made, 1)

            @block.vector
            def _(dve):
                dve.wait_ge(weights_in, 16 * (len(loads0) + len(loads1)))
                for k, a in enumerate((a1_sb[:, 0:1], a1_sb[:, 1:2], a3_sb[:, 0:1], a3_sb[:, 1:2])):
                    last = nc.vector.tensor_scalar(a_rep[:, k, :], ones[:, :], a, None, ALU.mult)
                last.then_inc(reps_made, 1)
                dve.wait_ge(wT_made, 1)
                nc.vector.tensor_copy(w1T[:, :], ps[:, 0, 0:P])
                nc.vector.tensor_copy(w3T[:, :], ps[:, 1, 0:P]).then_inc(wT_kept, 1)
                dve.wait_ge(v_made, 1)
                nc.vector.tensor_copy(v_rep[:, 0:2, :], ps[:, 2, 0:2 * P].rearrange("p (k q) -> p k q", k=2))
                nc.vector.tensor_copy(v_rep[:, 2:4, :], ps[:, 3, 0:2 * P].rearrange("p (k q) -> p k q", k=2))

        B_MAX, W_MAX = 100.0, 28.0
        LOG_X = 10 * float(np.log(2.0))
        PEN = 2048.0
        SPAN = float(D - 1)
        STEEP = 2.0 ** 64
        TINY = 1e-37
        PW = P + 1
        XW = 2 * PW
        MR = 4
        with ExitStack() as c_ctx:
            def sbc(name, shape, dt=fp32):
                return sb(name, shape, dt, c_ctx)

            def csem(name):
                return stage_sem(name)

            cases = ("A", "C")
            mask_A = sbc("mask_A", [P, 2, T, N], bf16)
            mask_C = sbc("mask_C", [P, 2, T, N], bf16)
            wts = mask_C[:, :, :, :].rearrange("p s t n -> p (s t n)").bitcast(fp32).rearrange("p (t n) -> p t n", t=T)
            masks = {"A": mask_A, "C": mask_C}
            ring = {x: sbc(f"ring_{x}", [P, MR, N], bf16) for x in cases}
            off = sbc("off", [P, 4, N], bf16)
            lk = sbc("lk", [P, 2, N])
            xA, xB, xC = sbc("xA", [P, T, P]), sbc("xB", [P, T, P]), sbc("xC", [P, T, P])
            qT = sbc("qT", [P, N])
            hN, hT = sbc("hN", [P, T, P]), sbc("hT_c", [P, N])
            s_row = {x: sbc(f"s_row_{x}", [P, N]) for x in cases}
            fac = {x: sbc(f"fac_{x}", [P, 2, T, XW], fp16) for x in cases}
            prod = sbc("prod", [P, 2, T, PW])
            hV = sbc("hV", [P, T, PW])
            hTB, ahB = sbc("hTB", [P, N]), sbc("ahB", [P, N])
            g_hi, g_lo, ag_hi, ag_lo = (sbc(n, [P, N], fp16) for n in ("g_hi", "g_lo", "ag_hi", "ag_lo"))
            up_part = sbc("up_part", [P, 2, XW])
            agg = sbc("agg", [P, T, XW])
            quo = sbc("quo", [P, T, PW])
            st_c = {x: sbc(f"st_{x}", [P, T, 6]) for x in "ABC"}
            mv_c = {x: sbc(f"mv_{x}", [P, T, 2]) for x in "ABC"}
            rs_c = {x: sbc(f"rs_{x}", [P, T]) for x in "ABC"}
            top = sbc("top", [P, 1])
            cols = sbc("cols", [P, T, 2])
            te, us = sbc("te", [P, T]), sbc("us", [P, T])
            arg = sbc("arg", [P, 4, T])
            steep_t = {x: sbc(f"steep_t_{x}", [P, T]) for x in cases}
            ex = {x: sbc(f"ex_{x}", [P, 4, T]) for x in cases}
            rec = sbc("rec", [P, T])
            recB = sbc("recB", [P, T])
            v2 = sbc("v2", [P, 2, 2])
            pen_id = sbc("pen_id", [P, P], bf16)
            a_row, a_top = sbc("a_row", [1, P]), sbc("a_top", [1, 1])
            wsq, wsum = sbc("wsq", [P, P]), sbc("wsum", [P, 2])
            shiftB, a2_use, w_fine = sbc("shiftB", [P, 1]), sbc("a2_use", [P, 1]), sbc("w_fine", [P, 1])
            w_use = sbc("w_use", [P, 2, P])
            mv_2, sc_2, sh_2, vr_2, rs_2 = sbc("mv_2", [P, 2]), sbc("sc_2", [P, 1]), sbc("sh_2", [P, 1]), sbc("vr_2", [P, 1]), sbc("rs_2", [P, 1])
            log_x = sbc("log_x", [P, 1])

            S = {}
            for x in cases:
                for n in ("var", "rstd", "h", "hT_made", "hT", "s_made", "s_row", "t_made", "top", "cols_made", "cols",
                          "args", "exp", "ind", "wh_made", "prod", "hi", "fac", "pos", "mask", "tile", "up", "agg", "done"):
                    S[x, n] = csem(f"{x}_{n}")
                S[x, "ring"] = [csem(f"{x}_ring{k}") for k in range(MR)]
            for n in ("q_in", "x_in", "q", "qT_made", "x1"):
                S["A", n] = csem(f"A_{n}")
            for n in ("neg", "neg_exp", "out"):
                S["C", n] = csem(f"C_{n}")
            for n in ("var", "rstd", "h", "hT_made", "hT", "hi", "ah", "ahi", "lo", "off", "gram", "exps", "wts", "tile",
                      "done"):
                S["B", n] = csem(f"B_{n}")
            S["B", "ring"] = [csem(f"B_ring{k}") for k in range(4)]
            (c_var, c_rstd, c_arow_made, c_atop, c_atop_made, c_norms, c_wok) = (csem(n) for n in (
                "c_var", "c_rstd", "c_arow_made", "c_atop", "c_atop_made", "c_norms", "c_wok"))

            def half(bank):
                return ps[:, bank:bank + 2, :]

            P_SLOTS = [half(4).rearrange("p a b -> p (a b)"), half(6).rearrange("p a b -> p (a b)")]
            Q_SLOTS = [half(0), half(2)]
            Q_FLAT = Q_SLOTS[0].rearrange("p a b -> p (a b)")

            with nc.Block() as block:
                @block.gpsimd
                def _(pool):
                    pool.wait_ge(c_var, 1)
                    pool.tensor_tensor(rs_2[:, :], vr_2[:, :], mhalf[:, 0:1], ALU.pow).then_inc(c_rstd, 1)

                @block.tensor
                def _(pe):
                    nc.tensor.transpose(ps[0:1, 0, 0:P], a2_sb[:, 0:1], ident[:, :]).then_inc(c_arow_made, 1)
                    pe.wait_ge(c_atop, 1)
                    nc.tensor.matmul(ps[:, 1, 0:1], ones[0:1, :], a_top[0:1, 0:1], start=True, stop=True).then_inc(c_atop_made, 1)
                    pe.wait_ge(c_norms, 1)
                    nc.tensor.matmul(ps[:, 2, 0:1], ones[:, :], w_fine[:, :], start=True, stop=True).then_inc(c_wok, 1)

                @block.vector
                def _(dve):
                    nc.vector.bn_aggr(mv_2[:, :], stats_2[:, :, :].rearrange("p n s -> p (n s)"))
                    dve.drain()
                    nc.vector.tensor_scalar(vr_2[:, :], mv_2[:, 1:2], BN_EPS, None, ALU.add).then_inc(c_var, 1)
                    dve.wait_ge(c_arow_made, 1)
                    nc.vector.tensor_reduce(a_top[0:1, 0:1], ps[0:1, 0, 0:P], AXX, ALU.max, apply_absolute_value=True).then_inc(c_atop, 1)
                    nc.vector.tensor_tensor(wsq[:, :], w1_sb[:, :], w1_sb[:, :], ALU.mult)
                    dve.drain()
                    nc.vector.tensor_reduce(wsum[:, 0:1], wsq[:, :], AXX, ALU.add)
                    dve.drain()
                    nc.vector.tensor_tensor(wsq[:, :], w3T[:, :], w3T[:, :], ALU.mult)
                    dve.drain()
                    nc.vector.tensor_reduce(wsum[:, 1:2], wsq[:, :], AXX, ALU.add)
                    nc.vector.tensor_scalar(pen_id[:, :], ident[:, :], PEN, None, ALU.mult)
                    nc.vector.memset(log_x[:, :], LOG_X)
                    nc.vector.memset(hV[:, :, :], 1.0)
                    nc.vector.memset(rec_top[:, :, :], 0.0)
                    for k, m in enumerate((1, 0, 3, 2)):
                        nc.vector.tensor_copy(v2[:, k // 2, k % 2:k % 2 + 1], v_rep[:, m, 0:1])
                    dve.wait_ge(c_atop_made, 1)
                    nc.vector.tensor_copy(bound_B[:, :], ps[:, 1, 0:1])
                    dve.drain()
                    nc.vector.tensor_scalar(bound_B[:, :], bound_B[:, :], SPAN, None, ALU.mult)
                    nc.vector.tensor_reduce(norm_W[:, :], wsum[:, :], AXX, ALU.max)
                    dve.wait_ge(c_rstd, 1)
                    nc.vector.tensor_tensor(sc_2[:, :], rs_2[:, :], g2_sb[:, :], ALU.mult)
                    dve.drain()
                    nc.vector.tensor_scalar(shiftB[:, :], bound_B[:, :], -0.4, None, ALU.mult)
                    nc.vector.tensor_scalar(a2_use[:, :], bound_B[:, :], B_MAX, None, ALU.is_le)
                    nc.vector.tensor_scalar(w_fine[:, :], norm_W[:, :], W_MAX, None, ALU.is_le)
                    dve.drain()
                    nc.vector.tensor_tensor(a2_use[:, :], a2_use[:, :], a2_sb[:, 0:1], ALU.mult).then_inc(c_norms, 1)
                    dve.wait_ge(c_wok, 1)
                    nc.vector.tensor_copy(w_fine[:, :], ps[:, 2, 0:1])
                    dve.drain()
                    nc.vector.tensor_scalar(w_fine[:, :], w_fine[:, :], P - 0.5, None, ALU.is_gt)
                    dve.drain()
                    nc.vector.tensor_scalar(w_use[:, 0, :], w1T[:, :], w_fine[:, 0:1], None, ALU.mult)
                    nc.vector.tensor_scalar(w_use[:, 1, :], w3_sb[:, :], w_fine[:, 0:1], None, ALU.mult)
                    nc.vector.tensor_tensor(sh_2[:, :], mv_2[:, 0:1], sc_2[:, :], ALU.mult)
                    dve.drain()
                    nc.vector.tensor_tensor(sh_2[:, :], be2_sb[:, :], sh_2[:, :], ALU.subtract)

            with nc.Block() as block:
                @block.sync
                def _(sp):
                    def load_mask(x, ring_x, slots, used, b, j):
                        if not (isinstance(b, int) and b == 0 and j < slots):
                            sp.wait_ge(used, b * T + j - slots + 1)
                        sp.dma_start(ring_x[:, j % slots, :], maskT_dram[bass.ds(b, 1), :, j, :].rearrange("a p n -> (a p) n")) \
                            .then_inc(S[x, "ring"][j % slots], 16)

                    def load_q(b):
                        if not (isinstance(b, int) and b == 0):
                            sp.wait_ge(S["A", "qT_made"], b)
                        sp.dma_start(qT[:, :], pTf_dram[bass.ds(b, 1)].rearrange("a p n -> (a p) n")).then_inc(S["A", "q_in"], 16)

                    def run(i, hasC, hasB, hasA, next_q):
                        if hasA:
                            if not isinstance(i, int) or i > 0:
                                sp.wait_ge(S["A", "done"], i)
                            sp.dma_start(xA[:, :, :], x_v[bass.ds(i, 1)].rearrange("a p t d -> (a p) t d")).then_inc(S["A", "x_in"], 16)
                        if hasB:
                            for j in range(4):
                                load_mask("B", off, 4, S["B", "gram"], i - 1, j)
                        if hasA:
                            for j in range(MR):
                                load_mask("A", ring["A"], MR, S["A", "mask"], i, j)
                        if hasB:
                            for j in range(4, 6):
                                load_mask("B", off, 4, S["B", "gram"], i - 1, j)
                        if hasB:
                            for j in range(6, T):
                                load_mask("B", off, 4, S["B", "gram"], i - 1, j)
                        if hasC:
                            sp.wait_ge(S["C", "done"], i - 1)
                            sp.dma_start(out_v[bass.ds(i - 2, 1)].rearrange("a p t d -> (a p) t d"), xC[:, :, :]).then_inc(S["C", "out"], 16)
                        if hasB:
                            for j in range(MR):
                                load_mask("C", ring["C"], MR, S["C", "mask"], i - 1, j)
                        if next_q:
                            load_q(i + 1)
                        if hasA:
                            for j in range(MR, T):
                                load_mask("A", ring["A"], MR, S["A", "mask"], i, j)
                        if hasB:
                            for j in range(MR, T):
                                load_mask("C", ring["C"], MR, S["C", "mask"], i - 1, j)

                    load_q(0)
                    run(0, False, False, True, True)
                    run(1, False, True, True, True)
                    with sp.Fori(2, B - 1) as i:
                        run(i, True, True, True, True)
                    run(B - 1, True, True, True, False)
                    run(B, True, True, False, False)
                    run(B + 1, True, False, False, False)
                    sp.wait_ge(S["C", "out"], B * 16)

                @block.gpsimd
                def _(pool):
                    def rstd(x, b):
                        pool.wait_ge(S[x, "var"], b + 1)
                        pool.tensor_tensor(rs_c[x][:, :], rs_c[x][:, :], mhalf[:, :], ALU.pow).then_inc(S[x, "rstd"], 1)

                    def run(i, hasC, hasB, hasA):
                        if hasB:
                            rstd("B", i - 1)
                        if hasA:
                            rstd("A", i)
                        if hasB:
                            rstd("C", i - 1)

                    run(0, False, False, True)
                    run(1, False, True, True)
                    with pool.Fori(2, B) as i:
                        run(i, True, True, True)
                    run(B, True, True, False)

                @block.vector
                def _(dve):
                    def stats(x, src, t):
                        nc.vector.bn_stats(st_c[x][:, t, :], src[:, t, :])

                    def moments(x):
                        dve.drain()
                        for t in range(T):
                            nc.vector.bn_aggr(mv_c[x][:, t, :], st_c[x][:, t, :])
                        dve.drain()
                        nc.vector.tensor_scalar(rs_c[x][:, :], mv_c[x][:, :, 1], LN_EPS, None, ALU.add).then_inc(S[x, "var"], 1)

                    def norm(x, b, src):
                        dve.drain()
                        for t in range(T):
                            nc.vector.bn_stats(st_c[x][:, t, :], src[:, t, :])
                        dve.drain()
                        for t in range(T):
                            nc.vector.bn_aggr(mv_c[x][:, t, :], st_c[x][:, t, :])
                        dve.drain()
                        nc.vector.tensor_scalar(rs_c[x][:, :], mv_c[x][:, :, 1], LN_EPS, None, ALU.add).then_inc(S[x, "var"], 1)

                    def normed(x, b, src, dst, relu):
                        dve.wait_ge(S[x, "rstd"], b + 1)
                        for t in range(T):
                            last = nc.vector.tensor_scalar(dst[:, t, 0:P], src[:, t, :], mv_c[x][:, t, 0:1], rs_c[x][:, t:t + 1],
                                                           ALU.subtract, ALU.mult)
                        if relu:
                            dve.drain()
                            last = nc.vector.tensor_scalar(dst[:, :, 0:P], dst[:, :, 0:P], 0.0, None, ALU.max)
                        last.then_inc(S[x, "h"], 1)

                    def highest(x, b, slot):
                        dve.wait_ge(S[x, "t_made"], b + 1)
                        nc.vector.reduce_max(top[:, :], P_SLOTS[slot], AXX).then_inc(S[x, "top"], 1)

                    def exponents(x, b, slot):
                        dve.wait_ge(S[x, "cols_made"], b + 1)
                        nc.vector.tensor_copy(cols[:, :, :].rearrange("p t k -> p (t k)"), P_SLOTS[slot][:, 0:2 * T]).then_inc(S[x, "cols"], 1)
                        dve.drain()
                        nc.vector.tensor_scalar(steep_t[x][:, :], cols[:, :, 0], STEEP, None, ALU.mult)
                        nc.vector.tensor_scalar(te[:, :], cols[:, :, 0], top[:, 0:1], None, ALU.subtract)
                        nc.vector.tensor_scalar(us[:, :], cols[:, :, 1], top[:, 0:1], 1.0 - SLOPE, ALU.add, ALU.mult)
                        dve.drain()
                        nc.vector.tensor_scalar(arg[:, 0, :], te[:, :], LOG_X, None, ALU.add)
                        nc.vector.tensor_scalar(arg[:, 1, :], te[:, :], SLOPE, LOG_X, ALU.mult, ALU.add)
                        nc.vector.tensor_scalar(arg[:, 2, :], us[:, :], 0.0, None, ALU.min)
                        nc.vector.tensor_scalar(arg[:, 3, :], us[:, :], -1.0, 0.0, ALU.mult, ALU.min).then_inc(S[x, "args"], 1)

                    def factors(x, b, slot):
                        dve.wait_ge(S[x, "exp"], b + 1)
                        dve.wait_ge(S[x, "wh_made"], b + 1)
                        wh = slot.rearrange("p (t d) -> p t d", t=T)
                        for k in range(2):
                            e = ex[x][:, k, :].unsqueeze(2)
                            nc.vector.tensor_copy(prod[:, k, :, P:PW], e)
                            last = nc.vector.tensor_tensor(prod[:, k, :, 0:P], wh, e.to_broadcast([P, T, P]), ALU.mult)
                            last.then_inc(S[x, "prod"], 1)

                    def low(x, b, k):
                        dve.wait_ge(S[x, "hi"], 2 * b + k + 1)
                        nc.vector.tensor_tensor(fac[x][:, k, :, PW:XW], prod[:, k, :, :], fac[x][:, k, :, 0:PW],
                                                ALU.subtract).then_inc(S[x, "fac"], 1)

                    def make_pos(x, b, j):
                        dve.wait_ge(S[x, "ring"][j % MR], (b * (T // MR) + j // MR + 1) * 16)
                        dve.wait_ge(S[x, "ind"], b * T + j + 1)
                        nc.vector.tensor_tensor(masks[x][:, 0, j, :], masks[x][:, 0, j, :], ring[x][:, j % MR, :],
                                                ALU.min).then_inc(S[x, "pos"], 1)

                    def make_neg(x, b, j):
                        dve.wait_ge(S[x, "pos"], b * T + j + 1)
                        nc.vector.tensor_tensor(masks[x][:, 1, j, :], ring[x][:, j % MR, :], masks[x][:, 0, j, :],
                                                ALU.subtract).then_inc(S[x, "mask"], 1)

                    def gather(x, b, c, q):
                        dve.wait_ge(S[x, "up"], b * T + c + 1)
                        nc.vector.scalar_tensor_tensor(agg[:, c, :], Q_SLOTS[q][:, 1, 0:XW], ex[x][:, 3, c:c + 1], up_part[:, c % 2, :],
                                                       ALU.mult, ALU.add).then_inc(S[x, "agg"], 1)

                    def quotients():
                        dve.drain()
                        nc.vector.tensor_tensor(quo[:, :, :], agg[:, :, 0:PW], agg[:, :, PW:XW], ALU.add)
                        dve.drain()
                        nc.vector.tensor_scalar(rec[:, :].unsqueeze(2), quo[:, :, P:PW], TINY, None, ALU.max)
                        dve.drain()
                        nc.vector.reciprocal(rec[:, :], rec[:, :])
                        dve.drain()

                    def off_tile(b, j):
                        dve.wait_ge(S["B", "ring"][j % 4], (b * (T // 4) + j // 4 + 1) * 16)
                        nc.vector.tensor_scalar(off[:, j % 4, :], off[:, j % 4, :], 1.0, 0.0, ALU.subtract, ALU.min).then_inc(S["B", "off"], 1)

                    def weights(b, j):
                        dve.wait_ge(S["B", "exps"], b * T + j + 1)
                        nc.vector.scalar_tensor_tensor(wts[:, j, :], lk[:, j % 2, :], 1.0, wts[:, j, :], ALU.max,
                                                       ALU.mult).then_inc(S["B", "wts"], 1)

                    def run(i, hasC, hasB, hasA):
                        if hasA:
                            dve.drain()
                            dve.wait_ge(S["A", "q_in"], i * 16 + 16)
                            nc.vector.tensor_scalar(qT[:, :], qT[:, :], sc_2[:, 0:1], sh_2[:, 0:1], ALU.mult, ALU.add).then_inc(S["A", "q"], 1)
                        if hasC:
                            gather("C", i - 2, 0, 0)
                        if hasB:
                            norm("B", i - 1, xB)
                        if hasC:
                            gather("C", i - 2, 1, 1)
                        if hasA:
                            dve.wait_ge(S["A", "x_in"], i * 16 + 16)
                            dve.wait_ge(S["A", "qT_made"], i + 1)
                            nc.vector.tensor_tensor(xA[:, :, :], xA[:, :, :], P_SLOTS[1].rearrange("p (t d) -> p t d", t=T),
                                                    ALU.add).then_inc(S["A", "x1"], 1)
                        if hasB:
                            normed("B", i - 1, xB, hV, True)
                        if hasC:
                            gather("C", i - 2, 2, 0)
                        if hasA:
                            norm("A", i, xA)
                        if hasC:
                            gather("C", i - 2, 3, 1)
                        if hasB:
                            for j in range(4):
                                off_tile(i - 1, j)
                        if hasA:
                            normed("A", i, xA, hN, False)
                        if hasC:
                            gather("C", i - 2, 4, 0)
                        if hasB:
                            dve.wait_ge(S["B", "hi"], i)
                            nc.vector.tensor_tensor(g_lo[:, :], hTB[:, :], g_hi[:, :], ALU.subtract)
                            dve.wait_ge(S["B", "ahi"], i)
                            nc.vector.tensor_tensor(ag_lo[:, :], ahB[:, :], ag_hi[:, :], ALU.subtract).then_inc(S["B", "lo"], 1)
                        if hasC:
                            gather("C", i - 2, 5, 1)
                        if hasA:
                            highest("A", i, 1)
                        if hasC:
                            gather("C", i - 2, 6, 0)
                        if hasA:
                            exponents("A", i, 0)
                        if hasC:
                            gather("C", i - 2, 7, 1)
                        if hasC:
                            quotients()
                            nc.vector.tensor_tensor(rec_top[:, 2, :], rec_top[:, 2, :], rec[:, :], ALU.max)
                        if hasB:
                            weights(i - 1, 0)
                        if hasC:
                            for c in range(T):
                                nc.vector.tensor_scalar(quo[:, c, 0:P], quo[:, c, 0:P], rec[:, c:c + 1], None, ALU.mult)
                            dve.drain()
                            nc.vector.tensor_scalar(agg[:, :, 0:P], quo[:, :, 0:P], 0.0, None, ALU.min).then_inc(S["C", "neg"], 1)
                        if hasB:
                            weights(i - 1, 1)
                            off_tile(i - 1, 4)
                        if hasA:
                            factors("A", i, Q_FLAT)
                        if hasB:
                            weights(i - 1, 2)
                            off_tile(i - 1, 5)
                        if hasC:
                            nc.vector.scalar_tensor_tensor(xC[:, :, :], quo[:, :, 0:P], 0.0, xC[:, :, :], ALU.max, ALU.add)
                            dve.drain()
                            dve.wait_ge(S["C", "neg_exp"], i - 1)
                            nc.vector.scalar_tensor_tensor(xC[:, :, :], agg[:, :, P:2 * P], -1.0, xC[:, :, :], ALU.add,
                                                           ALU.add).then_inc(S["C", "done"], 1)
                        if hasB:
                            weights(i - 1, 3)
                            off_tile(i - 1, 6)
                        if hasA:
                            low("A", i, 0)
                            low("A", i, 1)
                        if hasB:
                            weights(i - 1, 4)
                            off_tile(i - 1, 7)
                        if hasA:
                            make_pos("A", i, 0)
                        if hasB:
                            weights(i - 1, 5)
                        if hasA:
                            make_pos("A", i, 1)
                            make_neg("A", i, 0)
                        if hasB:
                            weights(i - 1, 6)
                        if hasA:
                            make_pos("A", i, 2)
                            make_neg("A", i, 1)
                        if hasB:
                            weights(i - 1, 7)
                        if hasB and (not isinstance(i, int) or i > 1):
                            dve.wait_ge(S["C", "out"], (i - 1) * 16)
                        for c in range(T):
                            if hasA and c + 2 < T:
                                if c + 3 < T:
                                    make_pos("A", i, c + 3)
                                make_neg("A", i, c + 2)
                            if hasB:
                                dve.wait_ge(S["B", "tile"], (i - 1) * T + c + 1)
                                nc.vector.tensor_scalar(recB[:, c:c + 1], Q_SLOTS[c % 2][:, 0, P:PW], TINY, None, ALU.max)
                                dve.drain()
                                nc.vector.reciprocal(recB[:, c:c + 1], recB[:, c:c + 1])
                                if c > 0:
                                    stats("C", xC, c - 1)
                                dve.drain()
                                last = nc.vector.scalar_tensor_tensor(xC[:, c, :], Q_SLOTS[c % 2][:, 0, 0:P], recB[:, c:c + 1], xB[:, c, :],
                                                                      ALU.mult, ALU.add)
                                last.then_inc(S["B", "done"], 1)
                        if hasB:
                            nc.vector.tensor_tensor(rec_top[:, 1, :], rec_top[:, 1, :], recB[:, :], ALU.max)
                        if hasB:
                            dve.drain()
                            stats("C", xC, T - 1)
                            moments("C")
                        if hasA:
                            gather("A", i, 0, 0)
                        if hasB:
                            normed("C", i - 1, xC, hN, False)
                        for c in range(1, T):
                            if hasA:
                                gather("A", i, c, c % 2)
                            if c == 4 and hasB:
                                highest("C", i - 1, 1)
                            if c == 5 and hasB:
                                exponents("C", i - 1, 0)
                            if c == 6 and hasB:
                                make_pos("C", i - 1, 0)
                                factors("C", i - 1, P_SLOTS[1])
                        if hasB:
                            low("C", i - 1, 0)
                            make_pos("C", i - 1, 1)
                            low("C", i - 1, 1)
                            make_neg("C", i - 1, 0)
                            for c in range(1, T):
                                if c + 1 < T:
                                    make_pos("C", i - 1, c + 1)
                                make_neg("C", i - 1, c)
                        if hasA:
                            quotients()
                            nc.vector.tensor_tensor(rec_top[:, 0, :], rec_top[:, 0, :], rec[:, :], ALU.max)
                            for c in range(T):
                                last = nc.vector.scalar_tensor_tensor(xB[:, c, :], quo[:, c, 0:P], rec[:, c:c + 1], xA[:, c, :],
                                                                      ALU.mult, ALU.add)
                            last.then_inc(S["A", "done"], 1)

                    run(0, False, False, True)
                    run(1, False, True, True)
                    with dve.Fori(2, B) as i:
                        run(i, True, True, True)
                    run(B, True, True, False)
                    run(B + 1, True, False, False)

                @block.scalar
                def _(act):
                    def up(x, b, c, q, before):
                        act.wait_ge(S[x, "tile"], b * T + c + 1)
                        if c >= 2:
                            act.wait_ge(S[x, "agg"], b * T + c - 1)
                        elif before:
                            act.wait_ge(S[before[0], "agg"], (before[1] + 1) * T + c - 1)
                        nc.scalar.mul(up_part[:, c % 2, :], Q_SLOTS[q][:, 0, 0:XW], ex[x][:, 2, c:c + 1]).then_inc(S[x, "up"], 1)

                    def relu_hT(x, b, slot):
                        act.wait_ge(S[x, "hT_made"], b + 1)
                        nc.scalar.activation(hT[:, :], P_SLOTS[slot], ACT.Relu).then_inc(S[x, "hT"], 1)

                    def keep_s(x, b, slot):
                        act.wait_ge(S[x, "s_made"], b + 1)
                        if not (isinstance(b, int) and b == 0):
                            act.wait_ge(S[x, "ind"], b * T)
                        nc.scalar.copy(s_row[x][:, :], P_SLOTS[slot]).then_inc(S[x, "s_row"], 1)

                    def indicate(x, b, j):
                        if j == 0 and not (isinstance(b, int) and b == 0):
                            act.wait_ge(S[x, "tile"], b * T)
                        if j == 0:
                            act.wait_ge(S[x, "s_row"], b + 1)
                            if x == "C":
                                act.wait_ge(S["B", "tile"], (b + 1) * T)
                        nc.scalar.activation(masks[x][:, 0, j, :], s_row[x][:, :], ACT.Relu, bias=steep_t[x][:, j:j + 1],
                                             scale=STEEP).then_inc(S[x, "ind"], 1)

                    def exps(x, b):
                        act.wait_ge(S[x, "args"], b + 1)
                        nc.scalar.activation(ex[x][:, :, :], arg[:, :, :], ACT.Exp).then_inc(S[x, "exp"], 1)

                    def high(x, b, k):
                        act.wait_ge(S[x, "prod"], 2 * b + k + 1)
                        nc.scalar.copy(fac[x][:, k, :, 0:PW], prod[:, k, :, :]).then_inc(S[x, "hi"], 1)

                    def score_exps(b, j):
                        act.wait_ge(S["B", "gram"], b * T + j + 1)
                        if j >= 2 or not (isinstance(b, int) and b == 0):
                            act.wait_ge(S["B", "wts"], b * T + j - 1)
                        nc.scalar.activation(lk[:, j % 2, :], P_SLOTS[j % 2], ACT.Exp, scale=1.0 - SLOPE)
                        nc.scalar.activation(wts[:, j, :], P_SLOTS[j % 2], ACT.Exp, bias=shiftB[:, 0:1],
                                             scale=SLOPE).then_inc(S["B", "exps"], 1)

                    def run(i, hasC, hasB, hasA):
                        for c in range(T):
                            if hasC:
                                up("C", i - 2, c, c % 2, ("A", i - 1) if hasB and hasA or not isinstance(i, int) or i == B else ("C", i - 3))
                            if c == 3 and hasB:
                                act.wait_ge(S["B", "hT_made"], i)
                                nc.scalar.copy(hTB[:, :], P_SLOTS[0]).then_inc(S["B", "hT"], 1)
                                act.wait_ge(S["B", "hT"], i)
                                nc.scalar.copy(g_hi[:, :], hTB[:, :]).then_inc(S["B", "hi"], 1)
                                nc.scalar.mul(ahB[:, :], hTB[:, :], a2_use[:, 0:1]).then_inc(S["B", "ah"], 1)
                                act.wait_ge(S["B", "ah"], i)
                                nc.scalar.copy(ag_hi[:, :], ahB[:, :]).then_inc(S["B", "ahi"], 1)
                            if c == 4 and hasA:
                                relu_hT("A", i, 1)
                            if c == 5 and hasA:
                                keep_s("A", i, 0)
                        if hasA:
                            exps("A", i)
                        if hasB:
                            score_exps(i - 1, 0)
                        if hasB:
                            score_exps(i - 1, 1)
                        if hasC:
                            act.wait_ge(S["C", "neg"], i - 1)
                            nc.scalar.activation(agg[:, :, P:2 * P], agg[:, :, 0:P], ACT.Exp).then_inc(S["C", "neg_exp"], 1)
                        if hasB:
                            score_exps(i - 1, 2)
                        if hasA:
                            high("A", i, 0)
                        if hasB:
                            score_exps(i - 1, 3)
                        if hasA:
                            high("A", i, 1)
                        if hasB:
                            score_exps(i - 1, 4)
                        if hasA:
                            indicate("A", i, 0)
                        if hasB:
                            score_exps(i - 1, 5)
                        if hasA:
                            indicate("A", i, 1)
                        if hasB:
                            score_exps(i - 1, 6)
                        if hasA:
                            indicate("A", i, 2)
                        if hasB:
                            score_exps(i - 1, 7)
                        if hasA:
                            for j in range(3, T):
                                indicate("A", i, j)
                        for c in range(T):
                            if hasA:
                                up("A", i, c, c % 2, ("C", i - 2) if hasC else ("A", i - 1) if hasB else None)
                            if c == 2 and hasB:
                                relu_hT("C", i - 1, 1)
                            if c == 3 and hasB:
                                keep_s("C", i - 1, 0)
                            if c == 5 and hasB:
                                exps("C", i - 1)
                                indicate("C", i - 1, 0)
                            if c == 6 and hasB:
                                high("C", i - 1, 0)
                        if hasB:
                            indicate("C", i - 1, 1)
                            high("C", i - 1, 1)
                            for j in range(2, T):
                                indicate("C", i - 1, j)

                    run(0, False, False, True)
                    run(1, False, True, True)
                    with act.Fori(2, B) as i:
                        run(i, True, True, True)
                    run(B, True, True, False)
                    run(B + 1, True, False, False)

                @block.tensor
                def _(pe):
                    free_p, free_q = [None, None], [None, None]

                    def take(free, slot, used, count):
                        if free[slot]:
                            pe.wait_ge(*free[slot])
                        free[slot] = (used, count)

                    def attend(x, b, c, q):
                        take(free_q, q, S[x, "agg"], b * T + c + 1)
                        if c == 0:
                            pe.wait_ge(S[x, "fac"], 2 * b + 2)
                        for k in range(2):
                            for j in range(T):
                                if c == 0 and k == 0:
                                    pe.wait_ge(S[x, "mask"], b * T + j + 1)
                                last = nc.tensor.matmul(Q_SLOTS[q][:, k, 0:XW], masks[x][:, k, j, c * P:c * P + P],
                                                        fac[x][:, k, j, :], start=(j == 0), stop=(j == T - 1))
                        last.then_inc(S[x, "tile"], 1)

                    def turn_h(x, b, src, slot, used):
                        take(free_p, slot, S[x, used], b + 1)
                        pe.wait_ge(S[x, "h"], b + 1)
                        for t in range(T):
                            last = nc.tensor.transpose(P_SLOTS[slot][:, t * P:t * P + P], src[:, t, 0:P], ident[:, :])
                        last.then_inc(S[x, "hT_made"], 1)

                    def project(x, b):
                        l = 0 if x == "A" else 1
                        take(free_p, 0, S[x, "s_row"], b + 1)
                        pe.wait_ge(S[x, "hT"], b + 1)
                        for c in range(CH):
                            last = nc.tensor.matmul(P_SLOTS[0][:, c * HALF:(c + 1) * HALF], v_rep[:, 2 * l, :],
                                                    hT[:, c * HALF:(c + 1) * HALF], start=True, stop=True)
                        last.then_inc(S[x, "s_made"], 1)
                        take(free_p, 1, S[x, "top"], b + 1)
                        for c in range(CH):
                            last = nc.tensor.matmul(P_SLOTS[1][:, c * HALF:(c + 1) * HALF], v_rep[:, 2 * l + 1, :],
                                                    hT[:, c * HALF:(c + 1) * HALF], start=True, stop=True)
                        last.then_inc(S[x, "t_made"], 1)

                    def columns(x, b):
                        l = 0 if x == "A" else 1
                        take(free_p, 0, S[x, "cols"], b + 1)
                        for t in range(T):
                            last = nc.tensor.matmul(P_SLOTS[0][:, 2 * t:2 * t + 2], hT[:, t * P:t * P + P], v2[:, l, :],
                                                    start=True, stop=True)
                        last.then_inc(S[x, "cols_made"], 1)

                    def values(x, b):
                        if x == "A":
                            take(free_q, 0, S[x, "prod"], 2 * b + 2)
                        else:
                            take(free_p, 1, S[x, "prod"], 2 * b + 2)
                        slot = Q_FLAT if x == "A" else P_SLOTS[1]
                        for t in range(T):
                            last = nc.tensor.matmul(slot[:, t * P:t * P + P], hT[:, t * P:t * P + P], w_use[:, cases.index(x), :],
                                                    start=True, stop=True)
                        last.then_inc(S[x, "wh_made"], 1)

                    def gram(b, j):
                        take(free_p, j % 2, S["B", "exps"], b * T + j + 1)
                        if j == 0:
                            pe.wait_ge(S["B", "lo"], b + 1)
                        pe.wait_ge(S["B", "off"], b * T + j + 1)
                        for c in range(CH):
                            cs = slice(c * HALF, (c + 1) * HALF)
                            js = slice(j * P, j * P + P)
                            nc.tensor.matmul(P_SLOTS[j % 2][:, cs], ag_hi[:, js], g_hi[:, cs], start=True, stop=False)
                            nc.tensor.matmul(P_SLOTS[j % 2][:, cs], ag_hi[:, js], g_lo[:, cs], start=False, stop=False)
                            nc.tensor.matmul(P_SLOTS[j % 2][:, cs], ag_lo[:, js], g_hi[:, cs], start=False, stop=False)
                            last = nc.tensor.matmul(P_SLOTS[j % 2][:, cs], pen_id[:, :], off[:, j % 4, cs], start=False, stop=True)
                        last.then_inc(S["B", "gram"], 1)

                    def weigh(b, c, q):
                        take(free_q, q, S["B", "done"], b * T + c + 1)
                        for j in range(T):
                            if c == 0:
                                pe.wait_ge(S["B", "wts"], b * T + j + 1)
                            last = nc.tensor.matmul(Q_SLOTS[q][:, 0, 0:PW], wts[:, j, c * P:c * P + P], hV[:, j, :],
                                                    start=(j == 0), stop=(j == T - 1))
                        last.then_inc(S["B", "tile"], 1)

                    def run(i, hasC, hasB, hasA):
                        for c in range(T):
                            if hasC:
                                attend("C", i - 2, c, c % 2)
                            if c == 1 and hasA:
                                take(free_p, 1, S["A", "x1"], i + 1)
                                pe.wait_ge(S["A", "q"], i + 1)
                                for t in range(T):
                                    last = nc.tensor.transpose(P_SLOTS[1][:, t * P:t * P + P], qT[:, t * P:t * P + P], ident[:, :])
                                last.then_inc(S["A", "qT_made"], 1)
                            if c == 3 and hasB:
                                turn_h("B", i - 1, hV, 0, "hT")
                            if c == 4 and hasA:
                                turn_h("A", i, hN, 1, "hT")
                            if c == 5 and hasA:
                                project("A", i)
                            if c == 6 and hasA:
                                columns("A", i)
                        if hasB:
                            gram(i - 1, 0)
                        if hasA:
                            values("A", i)
                        if hasB:
                            for j in range(1, T):
                                gram(i - 1, j)
                            for c in range(T):
                                weigh(i - 1, c, c % 2)
                        for c in range(T):
                            if hasA:
                                attend("A", i, c, c % 2)
                            if c == 2 and hasB:
                                turn_h("C", i - 1, hN, 1, "hT")
                            if c == 3 and hasB:
                                project("C", i - 1)
                            if c == 4 and hasB:
                                columns("C", i - 1)
                            if c == 5 and hasB:
                                values("C", i - 1)

                    def after(i):
                        free_p[0] = (S["C", "cols"], i)
                        free_p[1] = (S["C", "prod"], 2 * i)
                        free_q[0] = (S["A", "agg"], (i + 1) * T - 1)
                        free_q[1] = (S["A", "agg"], (i + 1) * T)

                    run(0, False, False, True)
                    run(1, False, True, True)
                    with pe.Fori(2, B) as i:
                        after(i - 1)
                        run(i, True, True, True)
                    after(B - 1)
                    run(B, True, True, False)
                    run(B + 1, True, False, False)

        retire_sems()

        limit = sb("limit", [P, 6])
        fine = sb("fine", [P, 1])
        apart = sb("apart", [P, NT])
        redo = sb("redo", [1, 1], i32)
        f_fine, f_sum, f_redo = sem("f_fine"), sem("f_sum"), sem("f_redo")
        REC_MAX = 64.0
        REC_B_MAX = 1e36
        with nc.Block() as block:
            @block.vector
            def _(dve):
                nc.vector.tensor_tensor(apart[:, :], sq_all[:, :], deg_all[:, :], ALU.subtract)
                dve.drain()
                nc.vector.tensor_reduce(limit[:, 0:1], apart[:, :], AXX, ALU.max, apply_absolute_value=True)
                nc.vector.reduce_max(limit[:, 1:2], r_top[:, :], AXX)
                nc.vector.reduce_max(limit[:, 2:3], rec_top[:, 0, :], AXX)
                nc.vector.reduce_max(limit[:, 3:4], rec_top[:, 2, :], AXX)
                nc.vector.reduce_max(limit[:, 4:5], rec_top[:, 1, :], AXX)
                nc.vector.reduce_max(limit[:, 5:6], spread[:, :], AXX)
                dve.drain()
                nc.vector.tensor_scalar(fine[:, :], limit[:, 0:1], 0.25, None, ALU.is_le)
                for value, most in ((limit[:, 1:2], ROW_MAX), (limit[:, 2:3], REC_MAX), (limit[:, 3:4], REC_MAX),
                                    (limit[:, 4:5], REC_B_MAX), (limit[:, 5:6], 1000.0), (bound_B[:, :], B_MAX),
                                    (norm_W[:, :], W_MAX)):
                    dve.drain()
                    last = nc.vector.scalar_tensor_tensor(fine[:, :], value, most, fine[:, :], ALU.is_le, ALU.mult)
                last.then_inc(f_fine, 1)
                dve.wait_ge(f_sum, 1)
                nc.vector.tensor_scalar(redo[0:1, 0:1], ps[0:1, 0, 0:1], P - 0.5, None, ALU.is_lt).then_inc(f_redo, 1)

            @block.tensor
            def _(pe):
                pe.wait_ge(f_fine, 1)
                nc.tensor.matmul(ps[0:1, 0, 0:1], fine[:, :], ones[:, 0:1], start=True, stop=True).then_inc(f_sum, 1)


        any_ctx = ctx.enter_context(ExitStack())

        def asb(name, shape, dt=fp32):
            return sb("any_" + name, shape, dt, any_ctx)

        def asem(name):
            return sem("any_" + name)

        xg, hg, cen = asb("xg", [P, T, P]), asb("hg", [P, T, P]), asb("cen", [P, T, P])
        lstat, lmv, lrs = asb("lstat", [P, T, 6]), asb("lmv", [P, T, 2]), asb("lrs", [P, T])
        adj_i = asb("adj_i", [P, N], i32)
        val, msk, sco, pro, tmp = (asb(n, [P, N]) for n in ("val", "msk", "sco", "pro", "tmp"))
        proT = asb("proT", [P, T, P])
        whT = asb("whT", [P, P])
        yT = asb("yT", [P, O2, P])
        yn = asb("yn", [P, O2, P])
        stats1 = asb("stats1", [P, O2, B * T, 6])
        stats2 = asb("stats2", [P, B * CH, 6])
        mv1, rs1 = asb("mv1", [P, O2, 2]), asb("rs1", [P, O2])
        sc1, sh1 = asb("sc1", [P, O2]), asb("sh1", [P, O2])
        mv2, rs2, sc2, sh2 = asb("mv2", [P, 1, 2]), asb("rs2", [P, 1]), asb("sc2", [P, 1]), asb("sh2", [P, 1])
        w_all = asb("w_all", [P, T, N])
        RK = asb("RK", [P, T, P])
        pT = asb("pT", [P, N])
        hT, Vn, Tb = asb("hT", [P, N]), asb("Vn", [P, T, P]), asb("Tb", [P, N])
        Sc = asb("Sc", [P, T])
        nmax, rsum, rinv, rok = asb("nmax", [P, 1]), asb("rsum", [P, 1]), asb("rinv", [P, 1]), asb("rok", [P, 1])
        si = asb("si", [P, 1])
        ah = asb("ah", [P, 4, P])
        neg_o, exp_o, pos_o = asb("neg_o", [P, P]), asb("exp_o", [P, P]), asb("pos_o", [P, P])

        x_loaded, var_ready, rstd_ready, h_ready = (asem(n) for n in ("x_loaded", "var_ready", "rstd_ready", "h_ready"))
        adj_loaded, adj_real, adjT_made = (asem(n) for n in ("adj_loaded", "adj_real", "adjT_made"))
        logits_ready, exp_ready, w_ready, w_saved = (asem(n) for n in ("logits_ready", "exp_ready", "w_ready", "w_saved"))
        wT_made, wT_ready, whT_made, whT_ready = (asem(n) for n in ("wT_made", "wT_ready", "whT_made", "whT_ready"))
        y_made, y_ready, y_saved = (asem(n) for n in ("y_made", "y_ready", "y_saved"))

        def any_norm_dve(dve, count):
            for t in range(T):
                nc.vector.bn_stats(lstat[:, t, :], xg[:, t, :])
            dve.drain()
            for t in range(T):
                nc.vector.bn_aggr(lmv[:, t, :], lstat[:, t, :])
            dve.drain()
            nc.vector.tensor_scalar(lrs[:, :], lmv[:, :, 1], LN_EPS, None, ALU.add).then_inc(var_ready, 1)
            dve.wait_ge(rstd_ready, count)
            for t in range(T):
                nc.vector.tensor_scalar(cen[:, t, :], xg[:, t, :], lmv[:, t, 0:1], lrs[:, t:t + 1], ALU.subtract, ALU.mult)
            dve.drain()
            nc.vector.tensor_scalar(hg[:, :, :], cen[:, :, :], 0.0, None, ALU.max).then_inc(h_ready, 1)

        with nc.allow_non_contiguous_dma("column blocks of adj"), nc.Block() as block:
            @block.sync
            def _(sp):
                with sp.If(sp.value_load(redo[0:1, 0:1]) != 0):
                    with sp.Fori(0, B) as b:
                        sp.wait_ge(y_saved, b * T * 16 + 16)
                        sp.dma_start(xg[:, :, :], x_v[b]).then_inc(x_loaded, 16)
                        with sp.Fori(0, T) as t:
                            n = b * T + t
                            sp.wait_ge(y_saved, n * 16 + 16)
                            sp.dma_start(adj_i[:, :].rearrange("p (t c) -> p t c", t=T),
                                         adj_cols[b, :, :, bass.ts(t, P)]).then_inc(adj_loaded, 16)
                            sp.wait_ge(w_ready, n + 1)
                            sp.dma_start(w_dram[b, bass.ts(t, P), :], pro[:, :]).then_inc(w_saved, 16)
                            sp.wait_ge(w_saved, n * 16 + 16)
                            sp.wait_ge(y_ready, n + 1)
                            sp.dma_start(y_dram[b, t], yT[:, :, :]).then_inc(y_saved, 16)
                    sp.wait_ge(y_saved, B * T * 16 + 16)
                sp.end_ifs()

            @block.gpsimd
            def _(pool):
                with pool.If(pool.value_load(redo[0:1, 0:1]) != 0):
                    pool.memset(nmax[:, :], 0.0).then_inc(y_saved, 16)
                    with pool.Fori(0, B) as b:
                        pool.wait_ge(var_ready, b + 1)
                        pool.tensor_tensor(lrs[:, :], lrs[:, :], mhalf[:, :], ALU.pow).then_inc(rstd_ready, 1)
                pool.end_ifs()

            @block.vector
            def _(dve):
                with dve.If(dve.value_load(redo[0:1, 0:1]) != 0):
                    with dve.Fori(0, B) as b:
                        dve.wait_ge(x_loaded, b * 16 + 16)
                        any_norm_dve(dve, b + 1)
                        with dve.Fori(0, T) as t:
                            n = b * T + t
                            dve.wait_ge(adj_loaded, n * 16 + 16)
                            nc.vector.tensor_copy(tmp[:, :], adj_i[:, :]).then_inc(adj_real, 1)
                            dve.wait_ge(adjT_made, n + 1)
                            nc.vector.tensor_copy(val[:, :], pair(0))
                            dve.drain()
                            nc.vector.tensor_scalar(msk[:, :], val[:, :], 0.0, None, ALU.not_equal)
                            dve.drain()
                            nc.vector.tensor_scalar(sco[:, :], msk[:, :], 1.0, NEG_SOFT, ALU.subtract, ALU.mult)
                            dve.drain()
                            nc.vector.tensor_tensor(sco[:, :], sco[:, :], val[:, :], ALU.add)
                            dve.drain()
                            nc.vector.reduce_max(nmax[:, :], sco[:, :], AXX, negate=True).then_inc(logits_ready, 1)
                            dve.wait_ge(exp_ready, n + 1)
                            nc.vector.reciprocal(rinv[:, :], rsum[:, :])
                            dve.drain()
                            nc.vector.scalar_tensor_tensor(pro[:, :], pro[:, :], rinv[:, 0:1], msk[:, :],
                                                           ALU.mult, ALU.mult).then_inc(w_ready, 1)
                            dve.wait_ge(y_made, n + 1)
                            for o in range(O2):
                                nc.vector.tensor_scalar(yT[:, o, :], ps[:, 5, o * P:o * P + P], b1_sb[:, o:o + 1], None, ALU.add)
                            dve.drain()
                            for o in range(O2):
                                last = nc.vector.bn_stats(stats1[:, o, bass.ds(n, 1), :].rearrange("p a s -> p (a s)"),
                                                          yT[:, o, :])
                            last.then_inc(y_ready, 1)
                dve.end_ifs()

            @block.scalar
            def _(act):
                with act.If(act.value_load(redo[0:1, 0:1]) != 0):
                    with act.Fori(0, B) as b:
                        with act.Fori(0, T) as t:
                            n = b * T + t
                            act.wait_ge(logits_ready, n + 1)
                            nc.scalar.activation(pro[:, :], sco[:, :], ACT.Exp, bias=nmax[:, 0:1],
                                                 accum_out=rsum[:, 0:1]).then_inc(exp_ready, 1)
                            act.wait_ge(wT_made, n + 1)
                            nc.scalar.copy(proT[:, :, :].rearrange("p t c -> p (t c)"), pair(1)).then_inc(wT_ready, 1)
                            act.wait_ge(whT_made, n + 1)
                            nc.scalar.copy(whT[:, :], ps[:, 4, 0:P]).then_inc(whT_ready, 1)
                act.end_ifs()

            @block.tensor
            def _(pe):
                with pe.If(pe.value_load(redo[0:1, 0:1]) != 0):
                    with pe.Fori(0, B) as b:
                        with pe.Fori(0, T) as t:
                            n = b * T + t
                            pe.wait_ge(adj_real, n + 1)
                            for r in range(T):
                                last = nc.tensor.transpose(pair(0)[:, r * P:r * P + P], tmp[:, r * P:r * P + P], ident[:, :])
                            last.then_inc(adjT_made, 1)
                            pe.wait_ge(w_ready, n + 1)
                            for r in range(T):
                                last = nc.tensor.transpose(pair(1)[:, r * P:r * P + P], pro[:, r * P:r * P + P], ident[:, :])
                            last.then_inc(wT_made, 1)
                            pe.wait_ge(wT_ready, n + 1)
                            for r in range(T):
                                last = nc.tensor.matmul(ps[:, 4, 0:P], hg[:, r, :], proT[:, r, :], start=(r == 0), stop=(r == T - 1))
                            last.then_inc(whT_made, 1)
                            pe.wait_ge(whT_ready, n + 1)
                            for o in range(O2):
                                last = nc.tensor.matmul(ps[:, 5, o * P:o * P + P], k1_sb[:, o * P:o * P + P], whT[:, :],
                                                        start=True, stop=True)
                            last.then_inc(y_made, 1)
                pe.end_ifs()

        var1, rstd1, w_in, y_in, yn_ready = (asem(n) for n in ("var1", "rstd1", "w_in", "y_in", "yn_ready"))
        rk_made, rk_ready, pT_made, pT_ready, pT_saved = (asem(n) for n in ("rk_made", "rk_ready", "pT_made", "pT_ready", "pT_saved"))

        with nc.Block() as block:
            @block.sync
            def _(sp):
                with sp.If(sp.value_load(redo[0:1, 0:1]) != 0):
                    with sp.Fori(0, B) as b:
                        sp.wait_ge(pT_saved, b * 16 + 16)
                        sp.dma_start(w_all[:, :, :], w_dram[b].rearrange("(t p) r -> p t r", p=P)).then_inc(w_in, 16)
                        with sp.Fori(0, T) as t:
                            sp.wait_ge(rk_made, b * T + t + 1)
                            sp.dma_start(yT[:, :, :], y_dram[b, t]).then_inc(y_in, 16)
                        sp.wait_ge(pT_ready, b + 1)
                        sp.dma_start(pT_dram[b], pT[:, :]).then_inc(pT_saved, 16)
                    sp.wait_ge(pT_saved, B * 16 + 16)
                sp.end_ifs()

            @block.gpsimd
            def _(pool):
                with pool.If(pool.value_load(redo[0:1, 0:1]) != 0):
                    pool.memset(nmax[:, :], 0.0).then_inc(pT_saved, 16)
                    pool.memset(rsum[:, :], 0.0).then_inc(rk_made, 1)
                    pool.wait_ge(var1, 1)
                    pool.tensor_tensor(rs1[:, :], rs1[:, :], mhalf[:, 0:O2], ALU.pow).then_inc(rstd1, 1)
                pool.end_ifs()

            @block.vector
            def _(dve):
                with dve.If(dve.value_load(redo[0:1, 0:1]) != 0):
                    for o in range(O2):
                        nc.vector.bn_aggr(mv1[:, o, :], stats1[:, o, :, :].rearrange("p n s -> p (n s)"))
                    dve.drain()
                    nc.vector.tensor_scalar(rs1[:, :], mv1[:, :, 1], BN_EPS, None, ALU.add).then_inc(var1, 1)
                    dve.wait_ge(rstd1, 1)
                    nc.vector.tensor_tensor(sc1[:, :], rs1[:, :], g1_sb[:, :], ALU.mult)
                    with dve.Fori(0, B) as b:
                        with dve.Fori(0, T) as t:
                            n = b * T + t
                            dve.drain()
                            dve.wait_ge(y_in, n * 16 + 16)
                            for o in range(O2):
                                nc.vector.tensor_scalar(yn[:, o, :], yT[:, o, :], mv1[:, o, 0:1], sc1[:, o:o + 1],
                                                        ALU.subtract, ALU.mult)
                            dve.drain()
                            for o in range(O2):
                                last = nc.vector.tensor_scalar(yn[:, o, :], yn[:, o, :], be1_sb[:, o:o + 1], None, ALU.add)
                            last.then_inc(yn_ready, 1)
                            dve.wait_ge(rk_made, n + 2)
                        dve.wait_ge(pT_made, b + 1)
                        nc.vector.tensor_scalar(pT[:, :], pair(1), b2_sb[:, 0:1], None, ALU.add)
                        dve.drain()
                        for c in range(CH):
                            last = nc.vector.bn_stats(stats2[:, bass.ds(b * CH + c, 1), :].rearrange("p a s -> p (a s)"),
                                                      pT[:, c * HALF:(c + 1) * HALF])
                        last.then_inc(pT_ready, 1)
                        dve.wait_ge(pT_saved, b * 16 + 32)
                dve.end_ifs()

            @block.scalar
            def _(act):
                with act.If(act.value_load(redo[0:1, 0:1]) != 0):
                    with act.Fori(0, B) as b:
                        with act.Fori(0, T) as t:
                            n = b * T + t
                            act.wait_ge(rk_made, n + 2)
                            nc.scalar.copy(RK[:, bass.ds(t, 1), :].rearrange("p a d -> p (a d)"), ps[:, 0, 0:P]).then_inc(rk_ready, 1)
                act.end_ifs()

            @block.tensor
            def _(pe):
                with pe.If(pe.value_load(redo[0:1, 0:1]) != 0):
                    with pe.Fori(0, B) as b:
                        with pe.Fori(0, T) as t:
                            n = b * T + t
                            pe.wait_ge(yn_ready, n + 1)
                            for o in range(O2):
                                last = nc.tensor.matmul(ps[:, 0, 0:P], yn[:, o, :], k2_sb[:, o, :], start=(o == 0), stop=(o == O2 - 1))
                            last.then_inc(rk_made, 1)
                            pe.wait_ge(rk_ready, n + 1)
                        pe.wait_ge(w_in, b * 16 + 16)
                        for c in range(CH):
                            for t in range(T):
                                last = nc.tensor.matmul(ps[:, 2 + c, :], RK[:, t, :], w_all[:, t, c * HALF:(c + 1) * HALF],
                                                        start=(t == 0), stop=(t == T - 1))
                        last.then_inc(pT_made, 1)
                pe.end_ifs()

        (var2, rstd2, g_loaded, q_ready, qT_made, var3, rstd3, hn_ready, hT_made, hT_ready, proj_made, V_ready,
         row_loaded, row_real, score_made, score_ready, score_used, lg_ready, ex_ready, at_ready, atT_made, atT_ready,
         o_made, neg_ready, elu_exp, tile_done, x_saved, ah_ready) = (asem(n) for n in (
            "var2", "rstd2", "g_loaded", "q_ready", "qT_made", "var3", "rstd3", "hn_ready", "hT_made", "hT_ready", "proj_made",
            "V_ready", "row_loaded", "row_real", "score_made", "score_ready", "score_used", "lg_ready", "ex_ready",
            "at_ready", "atT_made", "atT_ready", "o_made", "neg_ready", "elu_exp", "tile_done", "x_saved", "ah_ready"))
        LAYERS = 3

        with nc.Block() as block:
            @block.sync
            def _(sp):
                with sp.If(sp.value_load(redo[0:1, 0:1]) != 0):
                    with sp.Fori(0, B) as b:
                        sp.wait_ge(x_saved, b * 16 + 16)
                        sp.dma_start(xg[:, :, :], x_v[b]).then_inc(g_loaded, 16)
                        sp.dma_start(pT[:, :], pT_dram[b]).then_inc(g_loaded, 16)
                        for layer in range(LAYERS):
                            with sp.Fori(0, T) as t:
                                n = (b * LAYERS + layer) * T + t
                                sp.wait_ge(tile_done, n + 1)
                                sp.dma_start(adj_i[:, :], adj[b, bass.ts(t, P), :]).then_inc(row_loaded, 16)
                        sp.wait_ge(tile_done, (b + 1) * LAYERS * T + 1)
                        sp.dma_start(out_v[b], xg[:, :, :]).then_inc(x_saved, 16)
                    sp.wait_ge(x_saved, B * 16 + 16)
                sp.end_ifs()

            @block.gpsimd
            def _(pool):
                with pool.If(pool.value_load(redo[0:1, 0:1]) != 0):
                    pool.memset(si[:, :], 0.0).then_inc(x_saved, 16)
                    pool.memset(rok[:, :], 0.0).then_inc(tile_done, 1)
                    pool.wait_ge(var2, 1)
                    pool.tensor_tensor(rs2[:, :], rs2[:, :], mhalf[:, 0:1], ALU.pow).then_inc(rstd2, 1)
                    with pool.Fori(0, B * LAYERS) as m:
                        pool.wait_ge(var3, m + 1)
                        pool.tensor_tensor(lrs[:, :], lrs[:, :], mhalf[:, :], ALU.pow).then_inc(rstd3, 1)
                pool.end_ifs()

            def norm_dve(dve, count):
                for t in range(T):
                    nc.vector.bn_stats(lstat[:, t, :], xg[:, t, :])
                dve.drain()
                for t in range(T):
                    nc.vector.bn_aggr(lmv[:, t, :], lstat[:, t, :])
                dve.drain()
                nc.vector.tensor_scalar(lrs[:, :], lmv[:, :, 1], LN_EPS, None, ALU.add).then_inc(var3, 1)
                dve.wait_ge(rstd3, count)
                for t in range(T):
                    nc.vector.tensor_scalar(cen[:, t, :], xg[:, t, :], lmv[:, t, 0:1], lrs[:, t:t + 1],
                                            ALU.subtract, ALU.mult)
                dve.drain()
                nc.vector.tensor_scalar(hg[:, :, :], cen[:, :, :], 0.0, None, ALU.max).then_inc(hn_ready, 1)

            @block.vector
            def _(dve):
                with dve.If(dve.value_load(redo[0:1, 0:1]) != 0):
                    nc.vector.bn_aggr(mv2[:, 0, :], stats2[:, :, :].rearrange("p n s -> p (n s)"))
                    dve.drain()
                    nc.vector.tensor_scalar(rs2[:, :], mv2[:, :, 1], BN_EPS, None, ALU.add).then_inc(var2, 1)
                    dve.wait_ge(rstd2, 1)
                    nc.vector.tensor_tensor(sc2[:, :], rs2[:, :], g2_sb[:, :], ALU.mult)
                    with dve.Fori(0, B) as b:
                        dve.drain()
                        dve.wait_ge(g_loaded, b * 32 + 32)
                        nc.vector.tensor_scalar(pT[:, :], pT[:, :], mv2[:, 0, 0:1], sc2[:, 0:1], ALU.subtract, ALU.mult)
                        dve.drain()
                        nc.vector.tensor_scalar(pT[:, :], pT[:, :], be2_sb[:, 0:1], None, ALU.add).then_inc(q_ready, 1)
                        dve.wait_ge(qT_made, b + 1)
                        nc.vector.tensor_tensor(xg[:, :, :], xg[:, :, :], pair(0).rearrange("p (t d) -> p t d", t=T), ALU.add)
                        for layer in range(LAYERS):
                            m = b * LAYERS + layer
                            dve.drain()
                            norm_dve(dve, m + 1)
                            dve.wait_ge(V_ready, m + 1)
                            nc.vector.memset(rok[:, :], 1.0)
                            with dve.Fori(0, T) as t:
                                n = m * T + t
                                dve.wait_ge(row_loaded, n * 16 + 16)
                                nc.vector.tensor_copy(val[:, :], adj_i[:, :])
                                if layer == 1:
                                    dve.memset(sco[:, :], 0.0)
                                    nc.vector.memset(msk[:, :], 0.0)
                                    nc.vector.tensor_copy(si[:, :], Sc[:, bass.ds(t, 1)]).then_inc(row_real, 1)
                                    for k in range(4):
                                        dve.wait_ge(score_ready, (b * T + t) * 4 + k + 1)
                                        nc.vector.scalar_tensor_tensor(tmp[:, :], pro[:, :], SLOPE, pro[:, :],
                                                                       ALU.mult, ALU.max)
                                        dve.drain()
                                        nc.vector.scalar_tensor_tensor(tmp[:, :], val[:, :], float(k + 1), tmp[:, :],
                                                                       ALU.is_equal, ALU.mult)
                                        nc.vector.scalar_tensor_tensor(msk[:, :], val[:, :], float(k + 1), msk[:, :],
                                                                       ALU.is_equal, ALU.add)
                                        dve.drain()
                                        nc.vector.tensor_tensor(sco[:, :], sco[:, :], tmp[:, :], ALU.add).then_inc(score_used, 1)
                                else:
                                    nc.vector.tensor_copy(si[:, :], Sc[:, bass.ds(t, 1)])
                                    dve.drain()
                                    nc.vector.tensor_scalar(tmp[:, :], Tb[:, :], si[:, 0:1], None, ALU.add)
                                    nc.vector.tensor_scalar(msk[:, :], val[:, :], 0.0, None,
                                                            ALU.not_equal if layer == 0 else ALU.is_gt)
                                    dve.drain()
                                    nc.vector.scalar_tensor_tensor(sco[:, :], tmp[:, :], SLOPE, tmp[:, :], ALU.mult, ALU.max)
                                    dve.drain()
                                    nc.vector.tensor_tensor(sco[:, :], sco[:, :], msk[:, :], ALU.mult)
                                dve.drain()
                                nc.vector.tensor_scalar(tmp[:, :], msk[:, :], 1.0, NEG_BIG, ALU.subtract, ALU.mult)
                                dve.drain()
                                nc.vector.tensor_tensor(sco[:, :], sco[:, :], tmp[:, :], ALU.add)
                                dve.drain()
                                nc.vector.reduce_max(nmax[:, :], sco[:, :], AXX, negate=True).then_inc(lg_ready, 1)
                                dve.wait_ge(ex_ready, n + 1)
                                nc.vector.reciprocal(rinv[:, :], rsum[:, :])
                                if layer == 0:
                                    nc.vector.tensor_scalar(rok[:, :], nmax[:, :], NEG_BIG / 2, None, ALU.is_lt)
                                    dve.drain()
                                    nc.vector.tensor_tensor(rinv[:, :], rinv[:, :], rok[:, :], ALU.mult)
                                dve.drain()
                                nc.vector.tensor_scalar(pro[:, :], pro[:, :], rinv[:, 0:1], None, ALU.mult).then_inc(at_ready, 1)
                                dve.wait_ge(o_made, n + 1)
                                xt = xg[:, bass.ds(t, 1), :].rearrange("p a d -> p (a d)")
                                if layer < 2:
                                    nc.vector.tensor_copy(pos_o[:, :], ps[:, 2, 0:P])
                                    dve.drain()
                                else:
                                    nc.vector.tensor_scalar(neg_o[:, :], ps[:, 2, 0:P], 0.0, None, ALU.min)
                                    nc.vector.tensor_scalar(pos_o[:, :], ps[:, 2, 0:P], 0.0, None, ALU.max).then_inc(neg_ready, 1)
                                    dve.drain()
                                    dve.wait_ge(elu_exp, b * T + t + 1)
                                    nc.vector.scalar_tensor_tensor(pos_o[:, :], exp_o[:, :], -1.0, pos_o[:, :], ALU.add, ALU.add)
                                    dve.drain()
                                nc.vector.tensor_tensor(xt, xt, pos_o[:, :], ALU.add).then_inc(tile_done, 1)
                dve.end_ifs()

            @block.scalar
            def _(act):
                with act.If(act.value_load(redo[0:1, 0:1]) != 0):
                    with act.Fori(0, B) as b:
                        for layer in range(LAYERS):
                            m = b * LAYERS + layer
                            act.wait_ge(hT_made, m + 1)
                            nc.scalar.copy(hT[:, :], pair(0)).then_inc(hT_ready, 1)
                            act.wait_ge(proj_made, m + 1)
                            if layer == 1:
                                nc.scalar.copy(Sc[:, :], mhalf[:, :])
                                nc.scalar.copy(Vn[:, :, :], hg[:, :, :]).then_inc(V_ready, 1)
                            else:
                                nc.scalar.copy(Tb[:, :], pair(2))
                                nc.scalar.copy(Sc[:, :], ps[:, 6, 0:T])
                                nc.scalar.copy(Vn[:, :, :].rearrange("p t d -> p (t d)"), pair(1)).then_inc(V_ready, 1)
                            with act.Fori(0, T) as t:
                                n = m * T + t
                                if layer == 1:
                                    act.wait_ge(row_real, b * T + t + 1)
                                    for k in range(4):
                                        last = nc.scalar.mul(ah[:, k, :], hT[:, bass.ts(t, P)], a2_sb[:, k:k + 1])
                                    last.then_inc(ah_ready, 1)
                                    for k in range(4):
                                        act.wait_ge(score_made, (b * T + t) * 4 + k + 1)
                                        if k:
                                            act.wait_ge(score_used, (b * T + t) * 4 + k)
                                        nc.scalar.copy(pro[:, :], pair(k)).then_inc(score_ready, 1)
                                act.wait_ge(lg_ready, n + 1)
                                nc.scalar.activation(pro[:, :], sco[:, :], ACT.Exp, bias=nmax[:, 0:1],
                                                     accum_out=rsum[:, 0:1]).then_inc(ex_ready, 1)
                                act.wait_ge(atT_made, n + 1)
                                nc.scalar.copy(proT[:, :, :].rearrange("p t c -> p (t c)"), pair(0)).then_inc(atT_ready, 1)
                                if layer == 2:
                                    act.wait_ge(neg_ready, b * T + t + 1)
                                    nc.scalar.activation(exp_o[:, :], neg_o[:, :], ACT.Exp).then_inc(elu_exp, 1)
                act.end_ifs()

            @block.tensor
            def _(pe):
                with pe.If(pe.value_load(redo[0:1, 0:1]) != 0):
                    with pe.Fori(0, B) as b:
                        pe.wait_ge(q_ready, b + 1)
                        for t in range(T):
                            last = nc.tensor.transpose(pair(0)[:, t * P:t * P + P], pT[:, t * P:t * P + P], ident[:, :])
                        last.then_inc(qT_made, 1)
                        for layer in range(LAYERS):
                            m = b * LAYERS + layer
                            pe.wait_ge(hn_ready, m + 1)
                            for t in range(T):
                                last = nc.tensor.transpose(pair(0)[:, t * P:t * P + P], hg[:, t, :], ident[:, :])
                            last.then_inc(hT_made, 1)
                            pe.wait_ge(hT_ready, m + 1)
                            if layer != 1:
                                w = w1T if layer == 0 else w3_sb
                                v = 0 if layer == 0 else 2
                                for t in range(T):
                                    nc.tensor.matmul(pair(1)[:, t * P:t * P + P], hT[:, t * P:t * P + P], w[:, :], start=True, stop=True)
                                    nc.tensor.matmul(ps[:, 6, t:t + 1], hT[:, t * P:t * P + P], v_rep[:, v, 0:1], start=True, stop=True)
                                for c in range(CH):
                                    nc.tensor.matmul(ps[:, 4 + c, :], v_rep[:, v + 1, :], hT[:, c * HALF:(c + 1) * HALF],
                                                     start=True, stop=True)
                            nc.tensor.matmul(ps[:, 7, 0:1], ones[:, :], ones[:, 0:1], start=True, stop=True).then_inc(proj_made, 1)
                            with pe.Fori(0, T) as t:
                                n = m * T + t
                                if layer == 1:
                                    pe.wait_ge(ah_ready, b * T + t + 1)
                                    for k in range(4):
                                        for c in range(CH):
                                            last = nc.tensor.matmul(ps[:, 2 * k + c, :], ah[:, k, :], hT[:, c * HALF:(c + 1) * HALF],
                                                                    start=True, stop=True)
                                        last.then_inc(score_made, 1)
                                pe.wait_ge(at_ready, n + 1)
                                for r in range(T):
                                    last = nc.tensor.transpose(pair(0)[:, r * P:r * P + P], pro[:, r * P:r * P + P], ident[:, :])
                                last.then_inc(atT_made, 1)
                                pe.wait_ge(atT_ready, n + 1)
                                for r in range(T):
                                    last = nc.tensor.matmul(ps[:, 2, 0:P], proT[:, r, :], Vn[:, r, :], start=(r == 0), stop=(r == T - 1))
                                last.then_inc(o_made, 1)
                pe.end_ifs()


_INS = ['x', 'adj', 'L0_gnn_kernel_1', 'L0_gnn_bias_1', 'L0_gnn_gamma_1', 'L0_gnn_beta_1', 'L0_gnn_kernel_2',
        'L0_gnn_bias_2', 'L0_gnn_gamma_2', 'L0_gnn_beta_2', 'L1_gnn_W', 'L1_gnn_a', 'L2_gnn_a_0', 'L2_gnn_a_1',
        'L2_gnn_a_2', 'L2_gnn_a_3', 'L3_gnn_W', 'L3_gnn_a']


def kernel(**inputs):
    import numpy as _np
    import concourse.bacc as _bacc
    from concourse import mybir as _mybir
    from concourse.bass_utils import run_bass_kernel_spmd as _run

    nc = _bacc.Bacc("TRN2", target_bir_lowering=False, num_devices=1)
    arrays, args = {}, []
    for name in _INS:
        a = _np.ascontiguousarray(inputs[name])
        arrays[f"in_{name}"] = a
        args.append(nc.dram_tensor(f"in_{name}", a.shape, _mybir.dt.from_np(a.dtype), kind="ExternalInput").ap())
    args.append(nc.dram_tensor("out_0", inputs["x"].shape, _mybir.dt.float32, kind="ExternalOutput").ap())
    gnn_stack_kernel(nc, *args)
    r = _run(nc, [arrays], core_ids=[0])
    return r.results[0]["out_0"]
```
